# Optimizing a Trainium2 kernel written in Bass

```python
import numpy as np
import jax
import jax.numpy as jnp

def _softmax(x, axis=-1):
    return jax.nn.softmax(x, axis=axis)

def _gelu(x):
    return jax.nn.gelu(x, approximate=True)

def _silu(x):
    return jax.nn.silu(x)

def _sigmoid(x):
    return jax.nn.sigmoid(x)

def _layernorm(x, axis=-1, eps=1e-05):
    m = jnp.mean(x, axis=axis, keepdims=True)
    v = jnp.var(x, axis=axis, keepdims=True)
    return (x - m) / jnp.sqrt(v + eps)

def _scatter_add(tgt, idx, src, axis=0):
    return tgt.at[idx].add(src)

def _segment_sum(src, seg, n):
    return jax.ops.segment_sum(src, seg, n)
kernel_name = 'mk_adj_resnorm_d2_adj_r2_b7542e'

def setup_inputs(seed: int=0):
    np.random.seed(seed)
    _w = jnp.asarray

    def _rec_inputs():
        import jax
        import jax.numpy as jnp
        _gk = jax.random.key(seed)
        x = -0.000929 + 1 * jax.random.normal(jax.random.fold_in(_gk, 1), (8192, 128), jnp.float32)
        _w = (1.0 + jnp.arange(8192, dtype=jnp.float32)) ** (-0.5)
        _w = _w / _w.mean()
        _pij = jnp.clip(0.000488281 * _w[:, None] * _w[None, :], 0.0, 1.0)
        _a = jax.random.uniform(jax.random.fold_in(_gk, 2), (8192, 8192)) < _pij
        _a = jnp.logical_or(_a, jnp.eye(8192, dtype=bool))
        _af = _a.astype(jnp.float32)
        _af = _af * jax.random.uniform(jax.random.fold_in(_gk, 3), (8192, 8192), jnp.float32, 0.05, 1)
        adj = _af
        return (x, adj)
    x, adj = _rec_inputs()

    def _L0_gnn_setup():
        import jax, jax.numpy as jnp
        import numpy as np
        EPS = 1e-06
        key = jax.random.key(seed)
        k1, k2, k3 = jax.random.split(key, 3)
        N, F_IN, F_OUT = (4096, 128, 128)
        x = jax.random.normal(k1, (N, F_IN), dtype=jnp.float32)
        adj = jax.random.uniform(k2, (N, N), dtype=jnp.float32)
        stdv = 1.0 / np.sqrt(F_OUT)
        weight = jax.random.uniform(k3, (F_IN, F_OUT), dtype=jnp.float32, minval=-stdv, maxval=stdv)
        return {'x': x, 'adj': adj, 'weight': weight}
    _L0_gnn_all = _L0_gnn_setup()
    _L0_gnn_in = {k: v for k, v in _L0_gnn_all.items() if k in ('weight',)}
    del _L0_gnn_all

    def _L1_gnn_setup():
        import jax, jax.numpy as jnp
        import numpy as np
        N, DIM = (8192, 128)

        def _gru_cell(x, h, W_ih, W_hh, b_ih, b_hh):
            gi = x @ W_ih.T + b_ih
            gh = h @ W_hh.T + b_hh
            i_r, i_z, i_n = jnp.split(gi, 3, axis=-1)
            h_r, h_z, h_n = jnp.split(gh, 3, axis=-1)
            r = jax.nn.sigmoid(i_r + h_r)
            z = jax.nn.sigmoid(i_z + h_z)
            n = jnp.tanh(i_n + r * h_n)
            return (1.0 - z) * n + z * h
        key = jax.random.key(seed)
        ks = jax.random.split(key, 8)
        states = jax.random.normal(ks[0], (N, DIM), dtype=jnp.float32)
        adj = jax.random.uniform(ks[1], (N, N), dtype=jnp.float32)
        s = 1.0 / np.sqrt(DIM)
        W_msg = jax.random.uniform(ks[2], (DIM, DIM), minval=-s, maxval=s, dtype=jnp.float32)
        b_msg = jax.random.uniform(ks[3], (DIM,), minval=-s, maxval=s, dtype=jnp.float32)
        W_ih = jax.random.uniform(ks[4], (3 * DIM, DIM), minval=-s, maxval=s, dtype=jnp.float32)
        W_hh = jax.random.uniform(ks[5], (3 * DIM, DIM), minval=-s, maxval=s, dtype=jnp.float32)
        b_ih = jax.random.uniform(ks[6], (3 * DIM,), minval=-s, maxval=s, dtype=jnp.float32)
        b_hh = jax.random.uniform(ks[7], (3 * DIM,), minval=-s, maxval=s, dtype=jnp.float32)
        return {'states': states, 'adj': adj, 'W_msg': W_msg, 'b_msg': b_msg, 'W_ih': W_ih, 'W_hh': W_hh, 'b_ih': b_ih, 'b_hh': b_hh}
    _L1_gnn_all = _L1_gnn_setup()
    _L1_gnn_in = {k: v for k, v in _L1_gnn_all.items() if k in ('W_msg', 'b_msg', 'W_ih', 'W_hh', 'b_ih', 'b_hh')}
    del _L1_gnn_all
    return {'x': x, 'adj': adj, 'L0_gnn_weight': _L0_gnn_in['weight'], 'L1_gnn_W_msg': _L1_gnn_in['W_msg'], 'L1_gnn_b_msg': _L1_gnn_in['b_msg'], 'L1_gnn_W_ih': _L1_gnn_in['W_ih'], 'L1_gnn_W_hh': _L1_gnn_in['W_hh'], 'L1_gnn_b_ih': _L1_gnn_in['b_ih'], 'L1_gnn_b_hh': _L1_gnn_in['b_hh']}

def reference(x, adj, L0_gnn_weight, L1_gnn_W_msg, L1_gnn_b_msg, L1_gnn_W_ih, L1_gnn_W_hh, L1_gnn_b_ih, L1_gnn_b_hh):
    import jax
    import jax.numpy as jnp

    def _L0_gnn_ref(x, adj, weight):
        import jax, jax.numpy as jnp
        import numpy as np
        EPS = 1e-06
        N = adj.shape[0]
        a_tilde = adj + jnp.eye(N, dtype=adj.dtype)
        d_inv_sqrt = jax.lax.rsqrt(jnp.sum(adj, axis=1) + EPS)
        adj_norm = d_inv_sqrt[:, None] * a_tilde * d_inv_sqrt[None, :]
        support = x @ weight
        return adj_norm @ support

    def _L1_gnn_ref(states, adj, W_msg, b_msg, W_ih, W_hh, b_ih, b_hh):
        import jax, jax.numpy as jnp
        import numpy as np
        N, DIM = (8192, 128)

        def _gru_cell(x, h, W_ih, W_hh, b_ih, b_hh):
            gi = x @ W_ih.T + b_ih
            gh = h @ W_hh.T + b_hh
            i_r, i_z, i_n = jnp.split(gi, 3, axis=-1)
            h_r, h_z, h_n = jnp.split(gh, 3, axis=-1)
            r = jax.nn.sigmoid(i_r + h_r)
            z = jax.nn.sigmoid(i_z + h_z)
            n = jnp.tanh(i_n + r * h_n)
            return (1.0 - z) * n + z * h
        agg = adj @ states
        msg = jax.nn.relu(agg @ W_msg.T + b_msg)
        return _gru_cell(msg, states, W_ih, W_hh, b_ih, b_hh)
    x = _layernorm(x + _L0_gnn_ref(x, adj, L0_gnn_weight), axis=-1)
    x = _layernorm(x + _L1_gnn_ref(x, adj, L1_gnn_W_msg, L1_gnn_b_msg, L1_gnn_W_ih, L1_gnn_W_hh, L1_gnn_b_ih, L1_gnn_b_hh), axis=-1)
    return x

_drawn_inputs = setup_inputs


def setup_inputs(seed=0):
    import zlib

    import numpy as np

    out = dict(_drawn_inputs(seed))
    spreads = {}
    factors = {'L1_gnn_b_msg': 8.0, 'L1_gnn_b_ih': 3.22, 'L1_gnn_b_hh': 5.087}
    for name, (base, spread) in spreads.items():
        noise = np.random.default_rng([zlib.crc32(name.encode()), seed]).standard_normal(out[name].shape)
        drawn = base * np.exp(spread * noise) if base else spread * noise
        out[name] = jnp.asarray(drawn.astype(out[name].dtype))
    for name, factor in factors.items():
        out[name] = (out[name] * factor).astype(out[name].dtype)
    return out
```

```python
import concourse.bass as bass
from concourse import mybir
from contextlib import ExitStack



class Tally:

    def __init__(self, eng, name, start=0):
        self.eng = eng
        self.reg = eng.alloc_register(name)
        eng.reg_mov(self.reg, start)

    def now(self):
        return self.eng.snap(self.reg)

    def add(self, n):
        self.eng.reg_add(self.reg, self.reg, n)


class Chain:

    def __init__(self, eng, sem, name):
        self.eng, self.sem, self.tally, self.k, self.base = eng, sem, Tally(eng, name), 0, None

    def begin(self):
        self.k, self.base = 0, self.tally.now()

    def link(self, ins, wait=None):
        ins.then_inc(self.sem, 1)
        self.k += 1
        if wait:
            wait(self.eng, self.sem, self.base + self.k)
        else:
            self.eng.wait_ge(self.sem, self.base + self.k)

    def end(self):
        self.tally.add(self.k)


def gnn_resnorm_kernel(nc, adj_blocks, x_t, x, w0, wmsg_t, b_msg, wih_t, whh_t, b_ih, b_hh, out):
    f32, f32r = mybir.dt.float32, mybir.dt.float32r
    ALU, ACT = mybir.AluOpType, mybir.ActivationFunctionType

    D = 128
    N = x.shape[0]
    W = 1024
    NP = N // W
    NU = W // 128
    NS = NU // 2
    HALF = 512
    NB = HALF // 128
    RING1 = NP * (NP - 1)
    PROD1 = NP * (NP + 1) // 2
    LN_EPS, DEG_EPS = 1e-5, 1e-6
    BIAS = NU

    x_rows = x.rearrange("(t p) f -> p t f", p=128)
    out_rows = out.rearrange("(t p) f -> p t f", p=128)

    ctx = ExitStack()
    with ctx:
        def sb(name, shape, dt=f32, at=ctx):
            return at.enter_context(nc.sbuf_tensor(name, shape, dt))

        def sem(name):
            return ctx.enter_context(nc.semaphore(name))

        feat = sb("feat", [128, N // 128, 2, D])
        part = sb("part", [128, N])
        ring = sb("ring", [128, NS, 2, W])
        tall = sb("tall", [128, 2, HALF])
        y = sb("y", [128, 2, NB, D])
        xin = sb("xin", [128, NU, D])
        stats = sb("stats", [128, 2, NB, 6])
        mv = sb("mv", [128, 2, NB, 2])
        var = sb("var", [128, 2, NB, 1])
        rstd = sb("rstd", [128, 2, NB, 1])
        deg = sb("deg", [128, NU, 1])
        dinv = sb("dinv", [128, N // 128, 1])
        mhalf = sb("mhalf", [128, NU, 1])
        ones = sb("ones", [128, 1])
        zeros = sb("zeros", [1, HALF], mybir.dt.bfloat16)
        ident = sb("ident", [128, 128])
        w0_s = sb("w0_s", [128, D])
        wmsg_s = sb("wmsg_s", [128, D])
        wih_s = sb("wih_s", [128, 3 * D])
        whh_s = sb("whh_s", [128, 3 * D])
        bmsg_s = sb("bmsg_s", [128, 1])
        bih_s = sb("bih_s", [128, 3])
        bhh_s = sb("bhh_s", [128, 3])
        brz = sb("brz", [128, 2])
        weights = [(w0_s[:, :], w0), (wmsg_s[:, :], wmsg_t), (wih_s[:, :], wih_t), (whh_s[:, :], whh_t),
                   (bmsg_s[:, :], b_msg), (bih_s[:, :], b_ih), (bhh_s[:, :], b_hh)]
        NW = len(weights)
        eps_ln = sb("eps_ln", [128, NU, 1])
        with ExitStack() as early:
            diag = sb("diag", [128, NS, 2, W], at=early)
            colsum = sb("colsum", [128, 2, W], at=early)
            xt = sb("xt", [128, W], at=early)
            feat_stage = sb("feat_stage", [128, 4, D], at=early)
        a_hi = sb("a_hi", [128, 4, W], f32r)
        a_lo = sb("a_lo", [128, 4, W], f32r)
        f_hi = sb("f_hi", [128, 4, 2, D], f32r)
        f_lo = sb("f_lo", [128, 4, 2, D], f32r)
        x1t = sb("x1t", [128, 2, HALF])
        msgt = sb("msgt", [128, 2, HALF])
        gr = sb("gr", [128, HALF])
        gz = sb("gz", [128, HALF])
        gn = sb("gn", [128, HALF])

        bank = [ctx.enter_context(nc.psum_tensor(f"bank{i}", [128, HALF], f32)) for i in range(8)]
        acc0, acc1 = bank[0:2], bank[2:4]
        tr = bank[4:6]
        p_deg = bank[6]
        p_msg, p_tr, p_r, p_z, p_in, p_hn = bank[4], bank[5], bank[0], bank[1], bank[6], bank[7]

        ring_in = [sem(f"ring_in{s}") for s in range(NS)]
        diag_in = [sem(f"diag_in{s}") for s in range(NS)]
        xt_in, xin_in, weights_in = sem("xt_in"), sem("xin_in"), sem("weights_in")
        stored = [sem(f"stored{h}") for h in range(2)]
        zeroed, consts = sem("zeroed"), sem("consts")
        sum_done = sem("sum_done")
        dsum_done = sem("dsum_done")
        cleared = sem("cleared")
        supp_done = sem("supp_done")
        deg_done = sem("deg_done")
        deg_ready = sem("deg_ready")
        dinv_ready = sem("dinv_ready")
        feat0_ready = sem("feat0_ready")
        staged = sem("staged")
        prod_done = sem("prod_done")
        part_ready = sem("part_ready")
        hi_ready, lo_ready = sem("hi_ready"), sem("lo_ready")
        done = [[sem(f"done{l}{h}") for h in range(2)] for l in range(2)]
        tall_ready = [sem(f"tall_ready{h}") for h in range(2)]
        kept = [sem(f"kept{h}") for h in range(2)]
        turned = [sem(f"turned{h}") for h in range(2)]
        turned_used = [sem(f"turned_used{h}") for h in range(2)]
        xin_used = sem("xin_used")
        var_ready, veps_ready, rstd_ready = sem("var_ready"), sem("veps_ready"), sem("rstd_ready")
        feat1_ready = sem("feat1_ready")
        agg_ready = [sem(f"agg_ready{h}") for h in range(2)]
        x1_ready, x1t_done, x1t_ready = sem("x1_ready"), sem("x1t_done"), sem("x1t_ready")
        msg_done, msg_ready = sem("msg_done"), sem("msg_ready")
        gates_done, rz_ready = sem("gates_done"), sem("rz_ready")
        npre_ready, n_ready = sem("npre_ready"), sem("n_ready")
        sum_ready, rows_done, rows_used = sem("sum_ready"), sem("rows_done"), sem("rows_used")
        y_ready = sem("y_ready")
        dve_chain = sem("dve_chain")
        passed = sem("passed")

        def wait_alone(eng, sem, value):
            eng.wait_ge(sem, value)
            eng.sem_inc(passed, 1)

        block = ctx.enter_context(nc.Block())

        @block.sync
        def _(sp):
            before = Tally(sp, "sp_before")

            def load(s, blk):
                sp.dma_start(ring[:, s], adj_blocks[bass.ds(blk, 1), s].rearrange("o p u c -> (o p) u c"))\
                  .then_inc(ring_in[s], 16)

            def ring_load1(n, at, products):
                for s in range(NS):
                    wait_alone(sp, sum_done, n * NS + (s + 1))
                    if products is not None:
                        wait_alone(sp, prod_done, products * NU + (2 * s + 2))
                    load(s, at)

            def panel(P, upper, lower):
                b = before.now() if lower else 0
                if upper:
                    with sp.Fori(0, NP - 1 - P) as k:
                        ring_load1(P * (NP - 1) + k, P * NP + (NP - 1 - k), b if lower else None)
                    if lower:
                        with sp.Fori(0, P) as t:
                            ring_load1(P * (NP - 2) + (t + (NP - 1)), P * (NP + 1) - t, b + (t + 1))
                else:
                    ring_load1(P * (NP - 1), P * (NP + 1), b)
                    with sp.Fori(1, P) as t:
                        ring_load1(t + P * (NP - 1), P * (NP + 1) - t, b + (t + 1))
                for s in range(NS):
                    if lower:
                        wait_alone(sp, prod_done, b * NU + (2 * s + 2 + NU))
                    sp.dma_start(diag[:, s], adj_blocks[bass.ds(P * NP, 1), s]
                                 .rearrange("o p u c -> (o p) u c")).then_inc(diag_in[s], 16)
                if lower:
                    before.add(P + 1)

            panel(0, True, False)
            with sp.Fori(1, NP - 1) as P:
                panel(P, True, True)
            panel(NP - 1, False, True)

            units = Tally(sp, "sp_units", NU)

            def ring_load(blk, first=False):
                u = 0 if first else units.now()
                for s in range(NS):
                    if first:
                        sp.wait_ge(sum_done, RING1 * NS + s + 1)
                        sp.wait_ge(prod_done, (PROD1 - 1) * NU + 2 * s + 2)
                    else:
                        wait_alone(sp, lo_ready, u + (2 * s + 2 - NU))
                    load(s, blk)
                if not first:
                    units.add(NU)

            ring_load((NP - 2) * NP + NP - 1, first=True)
            with sp.Fori(0, NP - 2) as i:
                with sp.Fori(NP - 2 - i, NP) as k:
                    ring_load((NP - 3 - i) * NP + k)
            with sp.Fori(0, NP) as i:
                with sp.Fori(0, NP - i) as k:
                    ring_load((NP - 1 - i) * NP + k)

        @block.tensor
        def _(pe):
            blocks1 = Tally(pe, "pe_blocks1")

            def product1(c, src, ready, value):
                for q in range(NU):
                    if q % 2 == 0:
                        pe.wait_ge(ready[q // 2], value)
                    pe.wait_ge(staged, c * NU + (q + 1))
                    for h in range(2):
                        mm = pe.matmul(acc0[h][:, :], feat_stage[:, q % 4, :],
                                       src[:, q // 2, q % 2, h * HALF:(h + 1) * HALF],
                                       start=False, stop=True, skip_group_check=True)
                    mm.then_inc(prod_done, 1)

            def panel1(P, lower):
                c = blocks1.now()
                pe.wait_ge(xt_in, P * 16 + 16)
                for b in range(NU):
                    mm = pe.matmul(tr[b // NB][:, (b % NB) * D:(b % NB + 1) * D], xt[:, b * 128:(b + 1) * 128],
                                   w0_s[:, :], start=True, stop=True)
                mm.then_inc(supp_done, 1)
                if lower:
                    pe.wait_ge(part_ready, P * 2)
                for h in range(2):
                    pe.matmul(acc0[h][:, :], zeros[0:1, 0:128], zeros[0:1, :], start=True, stop=True)
                if lower:
                    with pe.Fori(0, P) as t:
                        product1(c + t, ring, ring_in, (P * (NP - 2) + (NP + t)) * 16)
                pe.wait_ge(dsum_done, P * NS + NS)
                for b in range(NU):
                    for u in range(2):
                        mm = pe.matmul(p_deg[:, b:b + 1], colsum[:, u, b * 128:(b + 1) * 128], ones[:, :],
                                       start=u == 0, stop=u == 1)
                mm.then_inc(deg_done, 1)
                product1(c + P, diag, diag_in, P * 16 + 16)
                blocks1.add(P + 1)

            pe.wait_ge(consts, 2)
            pe.wait_ge(zeroed, 4)
            pe.wait_ge(weights_in, NW * 16)
            pe.matmul(acc0[0][:, 0:128], zeros[0:1, 0:128], zeros[0:1, 0:128], start=True, stop=True)\
              .then_inc(prod_done, BIAS)
            panel1(0, False)
            with pe.Fori(1, NP) as P:
                panel1(P, True)

            units = Tally(pe, "pe_units")

            def multiply(layers, begin, freed=None, steps={}):
                u = units.now()
                for q in range(NU):
                    pe.wait_ge(lo_ready, u + (q + 1))
                    for l in layers:
                        for h in range(2):
                            first = begin and q == 0
                            if first and freed:
                                freed(l, h)
                            cols = slice(h * HALF, (h + 1) * HALF)
                            acc = (acc0, acc1)[l][h][:, :]
                            pe.matmul(acc, f_hi[:, q % 4, l, :], a_hi[:, q % 4, cols],
                                      start=first, stop=False, skip_group_check=True)
                            pe.matmul(acc, f_hi[:, q % 4, l, :], a_lo[:, q % 4, cols],
                                      start=False, stop=False, skip_group_check=True)
                            pe.matmul(acc, f_lo[:, q % 4, l, :], a_hi[:, q % 4, cols],
                                      start=False, stop=True, skip_group_check=True).then_inc(done[l][h], 1)
                    for step in steps.get(q, ()):
                        step()
                units.add(NU)

            def turn(h, p):
                pe.wait_ge(tall_ready[h], p + 1)
                if not isinstance(p, int) or p:
                    pe.wait_ge(turned_used[h], p)
                for b in range(NB):
                    t = pe.transpose(tr[h][:, b * 128:(b + 1) * 128], tall[:, h, b * 128:(b + 1) * 128], ident[:, :])
                t.then_inc(turned[h], 1)

            pe.wait_ge(feat0_ready, 2 * NP)
            turn(0, 0)
            turn(1, 0)
            pe.wait_ge(part_ready, 2 * NP)
            multiply((0, 1), True)
            with pe.Fori(0, NP - 2) as i:
                def freed2(l, h):
                    if l == 0:
                        pe.wait_ge(tall_ready[h], i + 2)
                    else:
                        pe.wait_ge(kept[h], i + 1)

                multiply((0, 1), True, freed2, {1: [lambda: turn(0, i + 1)], 2: [lambda: turn(1, i + 1)]})
                with pe.Fori(0, i + 1) as k:
                    multiply((0, 1), False)

            def x1_step(h, p):
                pe.wait_ge(x1_ready, p * 2 + (h + 1))
                if h == 1:
                    pe.wait_ge(x1t_ready, p * 2 + 1)
                for b in range(NB):
                    t = pe.transpose(p_tr[:, b * 128:(b + 1) * 128], xin[:, h * NB + b, :], ident[:, :])
                t.then_inc(x1t_done, 1)

            def msg_step(h, p):
                pe.wait_ge(agg_ready[h], p + 1)
                pe.matmul(p_msg[:, :], wmsg_s[:, :], tall[:, h, :], start=True, stop=True).then_inc(msg_done, 1)

            def gates_step(h, p):
                pe.wait_ge(msg_ready, p * 2 + (h + 1))
                pe.wait_ge(x1t_ready, p * 2 + (h + 1))
                if h == 1:
                    pe.wait_ge(npre_ready, p * 2 + 1)
                m, s = msgt[:, h, :], x1t[:, h, :]
                for g, bank_g in ((0, p_r), (1, p_z)):
                    pe.matmul(bank_g[:, :], wih_s[:, g * D:(g + 1) * D], m, start=True, stop=False)
                    pe.matmul(bank_g[:, :], whh_s[:, g * D:(g + 1) * D], s, start=False, stop=True)
                pe.matmul(p_in[:, :], wih_s[:, 2 * D:3 * D], m, start=True, stop=True)
                pe.matmul(p_hn[:, :], whh_s[:, 2 * D:3 * D], s, start=True, stop=True).then_inc(gates_done, 1)

            def rows_step(h, p):
                pe.wait_ge(sum_ready, p * 2 + (h + 1))
                if h == 0:
                    pe.wait_ge(x1t_ready, p * 2 + 2)
                else:
                    pe.wait_ge(rows_used, p * 2 + 1)
                for b in range(NB):
                    t = pe.transpose(p_tr[:, b * 128:(b + 1) * 128], tall[:, h, b * 128:(b + 1) * 128], ident[:, :])
                t.then_inc(rows_done, 1)

            def gru_steps(p):
                return {0: [lambda: x1_step(0, p), lambda: msg_step(0, p)], 1: [lambda: gates_step(0, p)],
                        2: [lambda: x1_step(1, p), lambda: msg_step(1, p)], 3: [lambda: gates_step(1, p)],
                        5: [lambda: rows_step(0, p)], 6: [lambda: rows_step(1, p)]}

            def freed3(p):
                return lambda l, h: pe.wait_ge(agg_ready[h], p + 1)

            multiply((1,), True, lambda l, h: pe.wait_ge(kept[h], NP - 1),
                     {1: [lambda: turn(0, NP - 1)], 2: [lambda: turn(1, NP - 1)]})
            with pe.Fori(0, NP - 1) as k:
                multiply((1,), False)
            for h in range(2):
                pe.wait_ge(turned_used[h], NP)
            with pe.Fori(0, NP - 2) as i:
                multiply((1,), True, freed3(i), gru_steps(i))
                with pe.Fori(0, NP - 2 - i) as k:
                    multiply((1,), False)
            multiply((1,), True, freed3(NP - 2), gru_steps(NP - 2))
            for q, steps in gru_steps(NP - 1).items():
                for step in steps:
                    step()

        @block.scalar
        def _(act):
            blocks1 = Tally(act, "act_blocks1")

            for dst, src in weights:
                act.dma_start(dst, src).then_inc(weights_in, 16)

            def stage1(c, T):
                for q in range(NU):
                    act.wait_ge(prod_done, c * NU + (q - 4 + 1 + BIAS))
                    act.activation(feat_stage[:, q % 4, :], feat[:, bass.ds(T * NU + q, 1), 0, :]
                                   .rearrange("p o f -> p (o f)"), ACT.Copy).then_inc(staged, 1)

            def panel1(P, lower):
                c = blocks1.now()
                if lower:
                    act.wait_ge(feat0_ready, P * 2)
                    with act.Fori(0, P) as t:
                        stage1(c + t, t)
                act.wait_ge(feat0_ready, P * 2 + 2)
                stage1(c + P, P)
                act.wait_ge(prod_done, (c + P) * NU + (NU + BIAS))
                for h in range(2):
                    act.activation(part[:, bass.ds(P * W + h * HALF, HALF)], acc0[h][:, :], ACT.Copy)\
                       .then_inc(part_ready, 1)
                blocks1.add(P + 1)

            panel1(0, False)
            with act.Fori(1, NP) as P:
                panel1(P, True)

            units = Tally(act, "act_units", NU)

            def split_hi(T, l0, first=False, steps={}):
                u = 0 if first else units.now()
                for q in range(NU):
                    if q % 2 == 0:
                        act.wait_ge(ring_in[q // 2], u * 2 + (RING1 + 1) * 16)
                    if q >= 4 or not first:
                        act.wait_ge(done[1][1], u + (q - 4 + 1))
                    act.activation(a_hi[:, q % 4, :], ring[:, q // 2, q % 2, :], ACT.Copy)
                    act.activation(f_hi[:, q % 4, l0:2, :], feat[:, bass.ds(T * NU + q, 1), l0:2, :]
                                   .rearrange("p o l f -> p (o l) f"), ACT.Copy).then_inc(hi_ready, 1)
                    for step in steps.get(q, ()):
                        step(u)
                if not first:
                    units.add(NU)

            def keep(P, h, p):
                def step(u):
                    act.wait_ge(done[1][h], u)
                    act.wait_ge(tall_ready[h], p + 1)
                    act.activation(part[:, bass.ds(P * W + h * HALF, HALF)], acc1[h][:, :], ACT.Copy)\
                       .then_inc(kept[h], 1)
                return step

            act.wait_ge(prod_done, PROD1 * NU + BIAS)
            act.wait_ge(feat1_ready, 2)
            split_hi(NP - 1, 0, first=True)
            with act.Fori(0, NP - 2) as i:
                split_hi(NP - 1, 0, steps={0: [keep(NP - 2 - i, 0, i + 1), keep(NP - 2 - i, 1, i + 1)]})
                act.wait_ge(feat1_ready, i * 2 + 4)
                with act.Fori(0, i + 1) as k:
                    split_hi(NP - 2 - k, 0)

            def x1t_step(h, p):
                def step(u):
                    act.wait_ge(x1t_done, p * 2 + (h + 1))
                    act.activation(x1t[:, h, :], p_tr[:, :], ACT.Copy).then_inc(x1t_ready, 1)
                    act.wait_ge(msg_done, p * 2 + (h + 1))
                    act.activation(msgt[:, h, :], p_msg[:, :], ACT.Relu, bias=bmsg_s[:, 0:1]).then_inc(msg_ready, 1)
                return step

            def rz_step(h, p):
                def step(u):
                    act.wait_ge(gates_done, p * 2 + (h + 1))
                    if h == 1:
                        act.wait_ge(sum_ready, p * 2 + 1)
                    act.activation(gr[:, :], p_r[:, :], ACT.Sigmoid, bias=brz[:, 0:1])
                    act.activation(gz[:, :], p_z[:, :], ACT.Sigmoid, bias=brz[:, 1:2]).then_inc(rz_ready, 1)
                return step

            def n_step(h, p):
                def step(u):
                    act.wait_ge(npre_ready, p * 2 + (h + 1))
                    act.activation(gn[:, :], gn[:, :], ACT.Tanh, bias=bih_s[:, 2:3]).then_inc(n_ready, 1)
                return step

            def gru_steps(p):
                return {1: [x1t_step(0, p)], 2: [rz_step(0, p)], 3: [x1t_step(1, p), n_step(0, p)],
                        4: [rz_step(1, p)], 5: [n_step(1, p)]}

            split_hi(NP - 1, 1, steps={0: [keep(0, 0, NP - 1), keep(0, 1, NP - 1)]})
            act.wait_ge(feat1_ready, 2 * NP)
            with act.Fori(0, NP - 1) as k:
                split_hi(NP - 2 - k, 1)
            with act.Fori(0, NP - 2) as i:
                split_hi(NP - 2 - i, 1, steps=gru_steps(i))
                with act.Fori(i, NP - 2) as k:
                    split_hi(NP - 3 - k, 1)
            split_hi(0, 1, steps=gru_steps(NP - 2))
            for q, steps in gru_steps(NP - 1).items():
                for step in steps:
                    step(None)

        @block.vector
        def _(dve):
            chain = Chain(dve, dve_chain, "dve_chain_at")

            dve.memset(zeros[:, :], 0.0)
            dve.memset(ones[:, :], 1.0).then_inc(zeroed, 1)
            dve.memset(mhalf[:, :, :], -0.5).then_inc(zeroed, 1)
            dve.memset(eps_ln[:, :, :], LN_EPS).then_inc(zeroed, 1)
            dve.wait_ge(weights_in, NW * 16)
            dve.tensor_tensor(brz[:, :], bih_s[:, 0:2], bhh_s[:, 0:2], ALU.add).then_inc(zeroed, 1)

            def add_up(tile, sem_done):
                cs = colsum[:, :, :].rearrange("p u c -> p (u c)")
                dve.tensor_tensor(cs, cs, tile.rearrange("p u c -> p (u c)"), ALU.add).then_inc(sem_done, 1)

            dve.memset(colsum[:, :, :], 0.0).then_inc(sum_done, NS)
            with dve.Fori(0, NP) as P:
                with dve.Fori(0, NP - 1) as k:
                    m = (P * (NP - 1) + k)
                    for s in range(NS):
                        dve.wait_ge(ring_in[s], m * 16 + 16)
                        dve.wait_ge(sum_done, m * NS + (NS + s))
                        add_up(ring[:, s], sum_done)
                dve.wait_ge(sum_done, P * ((NP - 1) * NS) + NP * NS)
                for s in range(NS):
                    dve.wait_ge(diag_in[s], P * 16 + 16)
                    if s:
                        dve.wait_ge(dsum_done, P * NS + s)
                    add_up(diag[:, s], dsum_done)
                dve.wait_ge(deg_done, P + 1)
                dve.tensor_scalar(deg[:, :, 0], p_deg[:, 0:NU], DEG_EPS, None, ALU.add).then_inc(deg_ready, 1)
                dve.memset(colsum[:, :, :], 0.0).then_inc(cleared, 1)
                dve.wait_ge(dinv_ready, P + 1)
                for h in range(2):
                    t0 = P * NU + h * NB
                    dve.tensor_tensor(feat[:, bass.ds(t0, NB), 0, :], tr[h][:, :].rearrange("p (b f) -> p b f", b=NB),
                                      dinv[:, bass.ds(t0, NB), :].to_broadcast([128, NB, D]), ALU.mult)\
                       .then_inc(feat0_ready, 1)
                wait_alone(dve, cleared, P + 1)

            units = Tally(dve, "dve_units", NU)

            def split_lo(T, l0, first=False, steps={}):
                u = 0 if first else units.now()
                chain.begin()
                for q in range(NU):
                    dve.wait_ge(hi_ready, u + (q + 1))
                    dve.tensor_tensor(a_lo[:, q % 4, :], ring[:, q // 2, q % 2, :], a_hi[:, q % 4, :].bitcast(f32),
                                      ALU.subtract)
                    dve.tensor_tensor(f_lo[:, q % 4, l0:2, :], feat[:, bass.ds(T * NU + q, 1), l0:2, :]
                                      .rearrange("p o l f -> p (o l) f"), f_hi[:, q % 4, l0:2, :].bitcast(f32),
                                      ALU.subtract).then_inc(lo_ready, 1)
                    for step in steps.get(q, ()):
                        step(u)
                chain.end()
                if not first:
                    units.add(NU)

            def norm_stats(h, rows, at):
                for b in range(NB):
                    last = dve.bn_stats(stats[:, h, b, :], rows(b))
                chain.link(last, wait_alone)
                for b in range(NB):
                    last = dve.bn_aggr(mv[:, h, b, :], stats[:, h, b, :])
                last.then_inc(var_ready, 1)

            def normalize(h, rows, to, at):
                dve.wait_ge(rstd_ready, at)
                for b in range(NB):
                    last = dve.tensor_scalar(to(b), rows(b), mv[:, h, b, 0:1], rstd[:, h, b, :],
                                             ALU.subtract, ALU.mult)
                return last

            def tall_step(P, h, p):
                def step(u):
                    wait_alone(dve, done[0][h], u)
                    dve.tensor_tensor(tall[:, h, :], part[:, bass.ds(P * W + h * HALF, HALF)], acc0[h][:, :],
                                      ALU.add).then_inc(tall_ready[h], 1)
                return step

            def rows_step(P, h, p):
                def step(u):
                    t0 = P * NU + h * NB
                    yh = y[:, h, :, :]
                    dve.wait_ge(turned[h], p + 1)
                    ins = dve.tensor_tensor(yh, feat[:, bass.ds(t0, NB), 0, :],
                                            tr[h][:, :].rearrange("p (b f) -> p b f", b=NB), ALU.add)
                    chain.link(ins)
                    ins = dve.tensor_tensor(yh, yh, dinv[:, bass.ds(t0, NB), :].to_broadcast([128, NB, D]), ALU.mult)
                    ins.then_inc(turned_used[h], 1)
                    dve.wait_ge(turned_used[h], p + 1)
                    dve.wait_ge(xin_in, p * 16 + 16)
                    chain.link(dve.tensor_tensor(yh, yh, xin[:, h * NB:(h + 1) * NB, :], ALU.add))
                    norm_stats(h, lambda b: y[:, h, b, :], None)
                return step

            def x1_step(P, h, p):
                def step(u):
                    t0 = P * NU + h * NB
                    normalize(h, lambda b: y[:, h, b, :],
                              lambda b: feat[:, bass.ds(t0 + b, 1), 1, :].rearrange("p o f -> p (o f)"),
                              p * 2 + (h + 1)).then_inc(feat1_ready, 1)
                return step

            def layer0_steps(P, p):
                return {0: [tall_step(P, 0, p), tall_step(P, 1, p)], 2: [rows_step(P, 0, p)],
                        3: [rows_step(P, 1, p), x1_step(P, 0, p)], 4: [x1_step(P, 1, p)]}

            dve.wait_ge(feat0_ready, 2 * NP)
            chain.begin()
            for h in range(2):
                dve.wait_ge(part_ready, 2 * NP)
                cols = slice((NP - 1) * W + h * HALF, (NP - 1) * W + (h + 1) * HALF)
                ins = dve.tensor_copy(tall[:, h, :], part[:, cols])
                ins.then_inc(tall_ready[h], 1)
                dve.wait_ge(tall_ready[h], 1)
                chain.link(dve.memset(part[:, cols], 0.0))
            for h in range(2):
                rows_step(NP - 1, h, 0)(0)
                x1_step(NP - 1, h, 0)(0)
            chain.end()
            dve.wait_ge(feat1_ready, 2)
            split_lo(NP - 1, 0, first=True)
            with dve.Fori(0, NP - 2) as i:
                split_lo(NP - 1, 0, steps=layer0_steps(NP - 2 - i, i + 1))
                wait_alone(dve, feat1_ready, i * 2 + 4)
                with dve.Fori(0, i + 1) as k:
                    split_lo(NP - 2 - k, 0)

            def agg_step(P, h, p):
                def step(u):
                    wait_alone(dve, done[1][h], u)
                    dve.tensor_tensor(tall[:, h, :], part[:, bass.ds(P * W + h * HALF, HALF)], acc1[h][:, :],
                                      ALU.add).then_inc(agg_ready[h], 1)
                return step

            def npre_step(h, p):
                def step(u):
                    dve.wait_ge(rz_ready, p * 2 + (h + 1))
                    chain.link(dve.scalar_tensor_tensor(gn[:, :], p_hn[:, :], bhh_s[:, 2:3], gr[:, :],
                                                        ALU.add, ALU.mult))
                    dve.tensor_tensor(gn[:, :], gn[:, :], p_in[:, :], ALU.add).then_inc(npre_ready, 1)
                return step

            def sum_step(h, p):
                def step(u):
                    t = tall[:, h, :]
                    dve.wait_ge(n_ready, p * 2 + (h + 1))
                    dve.wait_ge(x1t_ready, p * 2 + (h + 1))
                    chain.link(dve.tensor_tensor(t, x1t[:, h, :], gn[:, :], ALU.subtract))
                    chain.link(dve.tensor_tensor(t, t, gz[:, :], ALU.mult))
                    chain.link(dve.tensor_tensor(t, t, gn[:, :], ALU.add))
                    dve.tensor_tensor(t, t, x1t[:, h, :], ALU.add).then_inc(sum_ready, 1)
                return step

            def out_step(h, p):
                def step(u):
                    rows = lambda b: p_tr[:, b * 128:(b + 1) * 128]
                    dve.wait_ge(rows_done, p * 2 + (h + 1))
                    norm_stats(h, rows, None)
                    normalize(h, rows, lambda b: y[:, h, b, :], p * 2 + (2 * NP + h + 1)).then_inc(rows_used, 1)
                return step

            def gru_steps(P, p):
                return {0: [agg_step(P, 0, p), agg_step(P, 1, p)], 3: [npre_step(0, p)], 4: [sum_step(0, p)],
                        5: [npre_step(1, p)], 6: [sum_step(1, p), out_step(0, p)], 7: [out_step(1, p)]}

            split_lo(NP - 1, 1, steps=layer0_steps(0, NP - 1))
            dve.wait_ge(feat1_ready, 2 * NP)
            with dve.Fori(0, NP - 1) as k:
                split_lo(NP - 2 - k, 1)
            with dve.Fori(0, NP - 2) as i:
                split_lo(NP - 2 - i, 1, steps=gru_steps(NP - 1 - i, i))
                with dve.Fori(i, NP - 2) as k:
                    split_lo(NP - 3 - k, 1)
            split_lo(0, 1, steps=gru_steps(1, NP - 2))
            u = units.now()
            chain.begin()
            for q, steps in gru_steps(0, NP - 1).items():
                for step in steps:
                    step(u)
            chain.end()

        @block.gpsimd
        def _(pool):
            pool.memset(ident[:, :], 0.0).then_inc(consts, 0 + 1)
            pool.wait_ge(consts, 1)
            pool.affine_select(out=ident[:, :], in_=ident[:, :], compare_op=ALU.not_equal, fill=1.0,
                               base=0, pattern=[[-1, 128]], channel_multiplier=1).then_inc(consts, 1)
            pool.wait_ge(zeroed, 4)

            def load_xt(P):
                pool.dma_start(xt[:, :], x_t[:, bass.ds(P * W, W)]).then_inc(xt_in, 16)

            def degrees(P):
                pool.wait_ge(deg_ready, P + 1)
                pool.tensor_tensor(dinv[:, bass.ds(P * NU, NU), :], deg[:, :, :], mhalf[:, :, :], ALU.pow)\
                    .then_inc(dinv_ready, 1)

            load_xt(0)
            with pool.Fori(0, NP - 1) as P:
                pool.wait_ge(supp_done, P + 1)
                load_xt(P + 1)
                degrees(P)
            degrees(NP - 1)

            def deviation(h, at):
                pool.wait_ge(var_ready, at)
                pool.tensor_tensor(var[:, h, :, :], mv[:, h, :, 1:2], eps_ln[:, 0:NB, :], ALU.add).then_inc(veps_ready, 1)
                pool.wait_ge(veps_ready, at)
                pool.tensor_tensor(rstd[:, h, :, :], var[:, h, :, :], mhalf[:, 0:NB, :], ALU.pow).then_inc(rstd_ready, 1)

            with pool.Fori(0, NP) as p:
                pool.dma_start(xin[:, :, :], x_rows[:, bass.ds((NP - 1 - p) * NU, NU), :]).then_inc(xin_in, 16)
                for h in range(2):
                    deviation(h, p * 2 + (h + 1))
            pool.wait_ge(feat1_ready, 2 * NP)
            with pool.Fori(0, NP) as p:
                for h in range(2):
                    pool.tensor_copy(xin[:, h * NB:(h + 1) * NB, :], feat[:, bass.ds((NP - 1 - p) * NU + h * NB, NB), 1, :])\
                        .then_inc(x1_ready, 1)
                for h in range(2):
                    deviation(h, p * 2 + (2 * NP + h + 1))
                    pool.wait_ge(rows_used, p * 2 + (h + 1))
                    pool.dma_start(out_rows[:, bass.ds((NP - 1 - p) * NU + h * NB, NB), :], y[:, h, :, :])\
                        .then_inc(stored[h], 16)
                for h in range(2):
                    wait_alone(pool, stored[h], p * 16 + 16)


def kernel(x, adj, L0_gnn_weight, L1_gnn_W_msg, L1_gnn_b_msg, L1_gnn_W_ih, L1_gnn_W_hh, L1_gnn_b_ih, L1_gnn_b_hh):
    import numpy as np
    import concourse.bacc as bacc
    from concourse.bass_utils import run_bass_kernel_spmd

    W, NP, D = 1024, 8, 128
    a = np.asarray(adj).reshape(NP, W, NP, 4, 2, 128).transpose(0, 2, 3, 5, 4, 1)
    blocks = np.empty((NP * NP, 4, 128, 2, W), a.dtype)
    for P in range(NP):
        for k in range(NP):
            blocks[P * NP + k] = a[P, (P - k) % NP]
    c = np.ascontiguousarray
    arrays = {
        "adj_blocks": blocks,
        "x_t": c(np.asarray(x).T),
        "x": c(np.asarray(x)),
        "w0": c(np.asarray(L0_gnn_weight)),
        "wmsg_t": c(np.asarray(L1_gnn_W_msg).T),
        "b_msg": c(np.asarray(L1_gnn_b_msg).reshape(1, D).T),
        "wih_t": c(np.asarray(L1_gnn_W_ih).T),
        "whh_t": c(np.asarray(L1_gnn_W_hh).T),
        "b_ih": c(np.asarray(L1_gnn_b_ih).reshape(3, D).T),
        "b_hh": c(np.asarray(L1_gnn_b_hh).reshape(3, D).T),
    }
    nc = bacc.Bacc("TRN2", target_bir_lowering=False, num_devices=1)
    aps = {n: nc.dram_tensor(n, v.shape, mybir.dt.from_np(v.dtype), kind="ExternalInput").ap()
           for n, v in arrays.items()}
    out = nc.dram_tensor("out", (NP * W, D), mybir.dt.float32, kind="ExternalOutput").ap()
    gnn_resnorm_kernel(nc, **aps, out=out)
    return run_bass_kernel_spmd(nc, [arrays], core_ids=[0]).results[0]["out"]
```

```python
import concourse.bass as bass
from concourse import mybir
from contextlib import ExitStack



class Tally:

    def __init__(self, eng, name, start=0):
        self.eng = eng
        self.reg = eng.alloc_register(name)
        eng.reg_mov(self.reg, start)

    def now(self):
        return self.eng.snap(self.reg)

    def add(self, n):
        self.eng.reg_add(self.reg, self.reg, n)


class Chain:

    def __init__(self, eng, sem, name):
        self.eng, self.sem, self.tally, self.k, self.base = eng, sem, Tally(eng, name), 0, None

    def begin(self):
        self.k, self.base = 0, self.tally.now()

    def link(self, ins, wait=None):
        ins.then_inc(self.sem, 1)
        self.k += 1
        if wait:
            wait(self.eng, self.sem, self.base + self.k)
        else:
            self.eng.wait_ge(self.sem, self.base + self.k)

    def end(self):
        self.tally.add(self.k)


def gnn_resnorm_kernel(nc, adj_blocks, x_t, x, w0, wmsg_t, b_msg, wih_t, whh_t, b_ih, b_hh, out):
    f32, f32r = mybir.dt.float32, mybir.dt.float32r
    ALU, ACT = mybir.AluOpType, mybir.ActivationFunctionType

    D = 128
    N = x.shape[0]
    W = 1024
    NP = N // W
    NU = W // 128
    NS = NU // 2
    HALF = 512
    NB = HALF // 128
    RING1 = NP * (NP - 1)
    PROD1 = NP * (NP + 1) // 2
    LN_EPS, DEG_EPS = 1e-5, 1e-6
    BIAS = NU

    x_rows = x.rearrange("(t p) f -> p t f", p=128)
    out_rows = out.rearrange("(t p) f -> p t f", p=128)

    ctx = ExitStack()
    with ctx:
        def sb(name, shape, dt=f32, at=ctx):
            return at.enter_context(nc.sbuf_tensor(name, shape, dt))

        def sem(name):
            return ctx.enter_context(nc.semaphore(name))

        feat = sb("feat", [128, N // 128, 2, D])
        part = sb("part", [128, N])
        ring = sb("ring", [128, NS, 2, W])
        tall = sb("tall", [128, 2, HALF])
        y = sb("y", [128, 2, NB, D])
        xin = sb("xin", [128, NU, D])
        stats = sb("stats", [128, 2, NB, 6])
        mv = sb("mv", [128, 2, NB, 2])
        var = sb("var", [128, 2, NB, 1])
        rstd = sb("rstd", [128, 2, NB, 1])
        deg = sb("deg", [128, NU, 1])
        dinv = sb("dinv", [128, N // 128, 1])
        mhalf = sb("mhalf", [128, NU, 1])
        ones = sb("ones", [128, 1])
        zeros = sb("zeros", [1, HALF], mybir.dt.bfloat16)
        ident = sb("ident", [128, 128])
        w0_s = sb("w0_s", [128, D])
        wmsg_s = sb("wmsg_s", [128, D])
        wih_s = sb("wih_s", [128, 3 * D])
        whh_s = sb("whh_s", [128, 3 * D])
        bmsg_s = sb("bmsg_s", [128, 1])
        bih_s = sb("bih_s", [128, 3])
        bhh_s = sb("bhh_s", [128, 3])
        brz = sb("brz", [128, 2])
        weights = [(w0_s[:, :], w0), (wmsg_s[:, :], wmsg_t), (wih_s[:, :], wih_t), (whh_s[:, :], whh_t),
                   (bmsg_s[:, :], b_msg), (bih_s[:, :], b_ih), (bhh_s[:, :], b_hh)]
        NW = len(weights)
        eps_ln = sb("eps_ln", [128, NU, 1])
        with ExitStack() as early:
            diag = sb("diag", [128, NS, 2, W], at=early)
            colsum = sb("colsum", [128, 2, W], at=early)
            csum = sb("csum", [128, W], at=early)
            xt = sb("xt", [128, W], at=early)
            feat_stage = sb("feat_stage", [128, 4, D], at=early)
        a_hi = sb("a_hi", [128, 4, W], f32r)
        a_lo = sb("a_lo", [128, 4, W], f32r)
        f_parts = sb("f_parts", [128, 4, 2, 2, D], f32r)
        x1t = sb("x1t", [128, 2, HALF])
        rounded = x1t[:, :, :].rearrange("p h c -> p (h c)").rearrange("p (t f) -> p t f", f=D)
        msgt = sb("msgt", [128, 2, HALF])
        gr = sb("gr", [128, 2, HALF])
        gz = sb("gz", [128, 2, HALF])
        gn = sb("gn", [128, 2, HALF])

        bank = [ctx.enter_context(nc.psum_tensor(f"bank{i}", [128, HALF], f32)) for i in range(8)]
        acc0, acc1 = bank[0:2], bank[2:4]
        tr = bank[4:6]
        p_deg = bank[6]
        p_msg, p_tr, p_r, p_z, p_in, p_hn = bank[4], bank[5], bank[0], bank[1], bank[6], bank[7]

        ring_in = [sem(f"ring_in{s}") for s in range(NS)]
        diag_in = [sem(f"diag_in{s}") for s in range(NS)]
        xt_in, xin_in, weights_in = sem("xt_in"), sem("xin_in"), sem("weights_in")
        stored = [sem(f"stored{h}") for h in range(2)]
        zeroed, consts = sem("zeroed"), sem("consts")
        sum_done = sem("sum_done")
        dsum_done = sem("dsum_done")
        csum_ready = sem("csum_ready")
        supp_done = sem("supp_done")
        deg_done = sem("deg_done")
        deg_ready = sem("deg_ready")
        dinv_ready = sem("dinv_ready")
        feat0_ready = sem("feat0_ready")
        staged = sem("staged")
        prod_done = sem("prod_done")
        part_ready = sem("part_ready")
        hi_ready, lo_ready = sem("hi_ready"), sem("lo_ready")
        done = [[sem(f"done{l}{h}") for h in range(2)] for l in range(2)]
        tall_ready = [sem(f"tall_ready{h}") for h in range(2)]
        kept = [sem(f"kept{h}") for h in range(2)]
        turned = [sem(f"turned{h}") for h in range(2)]
        turned_used = [sem(f"turned_used{h}") for h in range(2)]
        xin_used = sem("xin_used")
        var_ready, veps_ready, rstd_ready = sem("var_ready"), sem("veps_ready"), sem("rstd_ready")
        feat1_ready = sem("feat1_ready")
        x1_rounded, x1_lo_kept, x1_hi_kept = sem("x1_rounded"), sem("x1_lo_kept"), sem("x1_hi_kept")
        agg_ready = [sem(f"agg_ready{h}") for h in range(2)]
        x1_ready, x1t_done, x1t_ready = sem("x1_ready"), sem("x1t_done"), sem("x1t_ready")
        msg_done, msg_ready = sem("msg_done"), sem("msg_ready")
        gates_done, rz_ready = sem("gates_done"), sem("rz_ready")
        npre_ready, n_ready = sem("npre_ready"), sem("n_ready")
        sum_ready, rows_done, rows_used = sem("sum_ready"), sem("rows_done"), sem("rows_used")
        y_ready = sem("y_ready")
        dve_chain = sem("dve_chain")
        passed = sem("passed")

        def wait_alone(eng, sem, value):
            eng.wait_ge(sem, value)
            eng.sem_inc(passed, 1)

        def part1(steps):
            return {q: s for q, s in steps.items() if q < NU}

        def part2(steps):
            return {q - NU: s for q, s in steps.items() if q >= NU}

        def tail(*epilogues):
            return [step for steps in epilogues for q in sorted(steps) for step in steps[q]]

        block = ctx.enter_context(nc.Block())

        @block.sync
        def _(sp):
            before = Tally(sp, "sp_before")

            def load(s, blk):
                sp.dma_start(ring[:, s], adj_blocks[bass.ds(blk, 1), s].rearrange("o p u c -> (o p) u c"))\
                  .then_inc(ring_in[s], 16)

            def ring_load1(n, at, products):
                for s in range(NS):
                    wait_alone(sp, sum_done, n * NS + (s + 1))
                    if products is not None:
                        wait_alone(sp, prod_done, products * NU + (2 * s + 2))
                    load(s, at)

            def load_diag(P, b):
                for s in range(NS):
                    if b is not None:
                        wait_alone(sp, prod_done, b * NU + (2 * s + 2 + NU))
                    sp.dma_start(diag[:, s], adj_blocks[bass.ds(P * NP, 1), s]
                                 .rearrange("o p u c -> (o p) u c")).then_inc(diag_in[s], 16)

            def panel(P, upper, lower):
                b = before.now()
                if upper:
                    with sp.Fori(0, NP - 1 - P) as k:
                        ring_load1(P * (NP - 1) + k, P * NP + (NP - 1 - k), b)
                else:
                    ring_load1(P * (NP - 1), P * (NP + 1), b)
                if lower:
                    with sp.Fori(0 if upper else 1, P - 1) as t:
                        ring_load1(P * (NP - 2) + (t + (NP - 1)), P * (NP + 1) - t, b + (t + 1))
                load_diag(P, b)
                ring_load1(P * (NP - 1) + (NP - 2), P * NP + 1, b + P)
                before.add(P + 1)

            with sp.Fori(0, NP - 2) as k:
                ring_load1(k, NP - 1 - k, None)
            load_diag(0, None)
            ring_load1(NP - 2, 1, None)
            panel(1, True, False)
            with sp.Fori(2, NP - 1) as P:
                panel(P, True, True)
            panel(NP - 1, False, True)

            units = Tally(sp, "sp_units", NU)

            def ring_load(blk, first=False):
                u = 0 if first else units.now()
                for s in range(NS):
                    if first:
                        sp.wait_ge(sum_done, RING1 * NS + s + 1)
                        sp.wait_ge(prod_done, (PROD1 - 1) * NU + 2 * s + 2)
                    else:
                        wait_alone(sp, lo_ready, u + (2 * s + 2 - NU))
                    load(s, blk)
                if not first:
                    units.add(NU)

            ring_load((NP - 2) * NP + NP - 1, first=True)
            with sp.Fori(0, NP - 2) as i:
                with sp.Fori(NP - 2 - i, NP) as k:
                    ring_load((NP - 3 - i) * NP + k)
            with sp.Fori(0, NP) as i:
                with sp.Fori(0, NP - i) as k:
                    ring_load((NP - 1 - i) * NP + k)

        @block.tensor
        def _(pe):
            blocks1 = Tally(pe, "pe_blocks1")

            def product1(c, src, ready, value):
                for q in range(NU):
                    if q % 2 == 0:
                        pe.wait_ge(ready[q // 2], value)
                    pe.wait_ge(staged, c * NU + (q + 1))
                    for h in range(2):
                        mm = pe.matmul(acc0[h][:, :], feat_stage[:, q % 4, :],
                                       src[:, q // 2, q % 2, h * HALF:(h + 1) * HALF],
                                       start=False, stop=True, skip_group_check=True)
                    mm.then_inc(prod_done, 1)

            def panel1(P, lower):
                c = blocks1.now()
                pe.wait_ge(xt_in, P * 16 + 16)
                for b in range(NU):
                    mm = pe.matmul(tr[b // NB][:, (b % NB) * D:(b % NB + 1) * D], xt[:, b * 128:(b + 1) * 128],
                                   w0_s[:, :], start=True, stop=True)
                mm.then_inc(supp_done, 1)
                if lower:
                    pe.wait_ge(part_ready, P * 2)
                for h in range(2):
                    pe.matmul(acc0[h][:, :], zeros[0:1, 0:128], zeros[0:1, :], start=True, stop=True)
                if lower:
                    with pe.Fori(0, P) as t:
                        product1(c + t, ring, ring_in, (P * (NP - 2) + (NP + t)) * 16)
                pe.wait_ge(csum_ready, P + 1)
                for b in range(NU):
                    mm = pe.matmul(p_deg[:, b:b + 1], csum[:, b * 128:(b + 1) * 128], ones[:, :], start=True, stop=True)
                mm.then_inc(deg_done, 1)
                product1(c + P, diag, diag_in, P * 16 + 16)
                blocks1.add(P + 1)

            pe.wait_ge(consts, 2)
            pe.wait_ge(zeroed, 4)
            pe.wait_ge(weights_in, NW * 16)
            pe.matmul(acc0[0][:, 0:128], zeros[0:1, 0:128], zeros[0:1, 0:128], start=True, stop=True)\
              .then_inc(prod_done, BIAS)
            panel1(0, False)
            with pe.Fori(1, NP) as P:
                panel1(P, True)

            units = Tally(pe, "pe_units")

            def multiply(layers, begin, freed=None, steps={}):
                u = units.now()
                for q in range(NU):
                    pe.wait_ge(lo_ready, u + (q + 1))
                    for l in layers:
                        for h in range(2):
                            first = begin and q == 0
                            if first and freed:
                                freed(l, h)
                            cols = slice(h * HALF, (h + 1) * HALF)
                            acc = (acc0, acc1)[l][h][:, :]
                            pe.matmul(acc, f_parts[:, q % 4, 1, l, :], a_hi[:, q % 4, cols],
                                      start=first, stop=False, skip_group_check=True)
                            pe.matmul(acc, f_parts[:, q % 4, 1, l, :], a_lo[:, q % 4, cols],
                                      start=False, stop=False, skip_group_check=True)
                            pe.matmul(acc, f_parts[:, q % 4, 0, l, :], a_hi[:, q % 4, cols],
                                      start=False, stop=True, skip_group_check=True).then_inc(done[l][h], 1)
                    for step in steps.get(q, ()):
                        step()
                units.add(NU)

            def turn(h, p):
                pe.wait_ge(tall_ready[h], p + 1)
                if not isinstance(p, int) or p:
                    pe.wait_ge(turned_used[h], p)
                for b in range(NB):
                    t = pe.transpose(tr[h][:, b * 128:(b + 1) * 128], tall[:, h, b * 128:(b + 1) * 128], ident[:, :])
                t.then_inc(turned[h], 1)

            pe.wait_ge(feat0_ready, 2 * NP)
            turn(0, 0)
            turn(1, 0)
            pe.wait_ge(part_ready, 2 * NP)
            multiply((0, 1), True)
            with pe.Fori(0, NP - 2) as i:
                def freed2(l, h):
                    if l == 0:
                        pe.wait_ge(tall_ready[h], i + 2)
                    else:
                        pe.wait_ge(kept[h], i + 1)

                multiply((0, 1), True, freed2, {0: [lambda: turn(0, i + 1), lambda: turn(1, i + 1)]})
                with pe.Fori(0, i + 1) as k:
                    multiply((0, 1), False)

            def x1_step(h, p):
                pe.wait_ge(x1_ready, p * 2 + (h + 1))
                if h == 1:
                    pe.wait_ge(x1t_ready, p * 2 + 1)
                for b in range(NB):
                    t = pe.transpose(p_tr[:, b * 128:(b + 1) * 128], xin[:, h * NB + b, :], ident[:, :])
                t.then_inc(x1t_done, 1)

            def msg_step(h, p):
                pe.wait_ge(agg_ready[h], p + 1)
                pe.matmul(p_msg[:, :], wmsg_s[:, :], tall[:, h, :], start=True, stop=True).then_inc(msg_done, 1)

            def gates_step(h, p):
                pe.wait_ge(msg_ready, p * 2 + (h + 1))
                pe.wait_ge(x1t_ready, p * 2 + (h + 1))
                if h == 1:
                    pe.wait_ge(npre_ready, p * 2 + 1)
                m, s = msgt[:, h, :], x1t[:, h, :]
                for g, bank_g in ((0, p_r), (1, p_z)):
                    pe.matmul(bank_g[:, :], wih_s[:, g * D:(g + 1) * D], m, start=True, stop=False)
                    pe.matmul(bank_g[:, :], whh_s[:, g * D:(g + 1) * D], s, start=False, stop=True)
                pe.matmul(p_in[:, :], wih_s[:, 2 * D:3 * D], m, start=True, stop=True)
                pe.matmul(p_hn[:, :], whh_s[:, 2 * D:3 * D], s, start=True, stop=True).then_inc(gates_done, 1)

            def rows_step(h, p):
                pe.wait_ge(sum_ready, p * 2 + (h + 1))
                if h == 0:
                    pe.wait_ge(x1t_ready, p * 2 + 2)
                else:
                    pe.wait_ge(rows_used, p * 2 + 1)
                for b in range(NB):
                    t = pe.transpose(p_tr[:, b * 128:(b + 1) * 128], tall[:, h, b * 128:(b + 1) * 128], ident[:, :])
                t.then_inc(rows_done, 1)

            def gru_steps(p):
                return {0: [lambda: x1_step(0, p), lambda: msg_step(0, p)],
                        2: [lambda: gates_step(0, p), lambda: x1_step(1, p), lambda: msg_step(1, p)],
                        4: [lambda: gates_step(1, p)], 8: [lambda: rows_step(0, p)], 11: [lambda: rows_step(1, p)]}

            def freed3(p):
                return lambda l, h: pe.wait_ge(agg_ready[h], p + 1)

            multiply((1,), True, lambda l, h: pe.wait_ge(kept[h], NP - 1),
                     {0: [lambda: turn(0, NP - 1)], 1: [lambda: turn(1, NP - 1)]})
            with pe.Fori(0, NP - 1) as k:
                multiply((1,), False)
            for h in range(2):
                pe.wait_ge(turned_used[h], NP)
            with pe.Fori(0, NP - 3) as i:
                multiply((1,), True, freed3(i), part1(gru_steps(i)))
                multiply((1,), False, None, part2(gru_steps(i)))
                with pe.Fori(0, NP - 3 - i) as k:
                    multiply((1,), False)
            multiply((1,), True, freed3(NP - 3), part1(gru_steps(NP - 3)))
            multiply((1,), False, None, part2(gru_steps(NP - 3)))
            multiply((1,), True, freed3(NP - 2), part1(gru_steps(NP - 2)))
            for step in tail(part2(gru_steps(NP - 2)), gru_steps(NP - 1)):
                step()

        @block.scalar
        def _(act):
            blocks1 = Tally(act, "act_blocks1")

            for dst, src in weights:
                act.dma_start(dst, src).then_inc(weights_in, 16)

            def stage1(c, T):
                for q in range(NU):
                    act.wait_ge(prod_done, c * NU + (q - 4 + 1 + BIAS))
                    act.activation(feat_stage[:, q % 4, :], feat[:, bass.ds(T * NU + q, 1), 0, :]
                                   .rearrange("p o f -> p (o f)"), ACT.Copy).then_inc(staged, 1)

            def panel1(P, lower):
                c = blocks1.now()
                if lower:
                    act.wait_ge(feat0_ready, P * 2)
                    with act.Fori(0, P) as t:
                        stage1(c + t, t)
                act.wait_ge(feat0_ready, P * 2 + 2)
                stage1(c + P, P)
                act.wait_ge(prod_done, (c + P) * NU + (NU + BIAS))
                for h in range(2):
                    act.activation(part[:, bass.ds(P * W + h * HALF, HALF)], acc0[h][:, :], ACT.Copy)\
                       .then_inc(part_ready, 1)
                blocks1.add(P + 1)

            panel1(0, False)
            with act.Fori(1, NP) as P:
                panel1(P, True)

            units = Tally(act, "act_units", NU)

            def split_hi(T, sweep, first=False, steps={}):
                u = 0 if first else units.now()
                for q in range(NU):
                    if q % 2 == 0:
                        act.wait_ge(ring_in[q // 2], u * 2 + (RING1 + 1) * 16)
                    if q >= 4 or not first:
                        act.wait_ge(done[1][1], u + (q - 4 + 1))
                    act.activation(a_hi[:, q % 4, :], ring[:, q // 2, q % 2, :], ACT.Copy)
                    to = f_parts[:, q % 4, 1, :, :] if sweep == 2 else f_parts[:, q % 4, :, 1, :]
                    act.activation(to, feat[:, bass.ds(T * NU + q, 1), :, :]
                                   .rearrange("p o l f -> p (o l) f"), ACT.Copy).then_inc(hi_ready, 1)
                    for step in steps.get(q, ()):
                        step(u)
                if not first:
                    units.add(NU)

            def keep(P, h, p):
                def step(u):
                    act.wait_ge(done[1][h], u)
                    act.wait_ge(tall_ready[h], p + 1)
                    act.activation(part[:, bass.ds(P * W + h * HALF, HALF)], acc1[h][:, :], ACT.Copy)\
                       .then_inc(kept[h], 1)
                return step

            act.wait_ge(prod_done, PROD1 * NU + BIAS)
            act.wait_ge(feat1_ready, 2)
            split_hi(NP - 1, 2, first=True)
            with act.Fori(0, NP - 2) as i:
                split_hi(NP - 1, 2, steps={2: [keep(NP - 2 - i, 0, i + 1), keep(NP - 2 - i, 1, i + 1)]})
                act.wait_ge(feat1_ready, i * 2 + 4)
                with act.Fori(0, i + 1) as k:
                    split_hi(NP - 2 - k, 2)

            def x1t_step(h, p):
                def step(u):
                    act.wait_ge(x1t_done, p * 2 + (h + 1))
                    act.activation(x1t[:, h, :], p_tr[:, :], ACT.Copy).then_inc(x1t_ready, 1)
                    act.wait_ge(msg_done, p * 2 + (h + 1))
                    act.activation(msgt[:, h, :], p_msg[:, :], ACT.Relu, bias=bmsg_s[:, 0:1]).then_inc(msg_ready, 1)
                return step

            def rz_step(h, p):
                def step(u):
                    act.wait_ge(gates_done, p * 2 + (h + 1))
                    act.activation(gr[:, h, :], p_r[:, :], ACT.Sigmoid, bias=brz[:, 0:1])
                    act.activation(gz[:, h, :], p_z[:, :], ACT.Sigmoid, bias=brz[:, 1:2], scale=-1.0)\
                       .then_inc(rz_ready, 1)
                return step

            def n_step(h, p):
                def step(u):
                    act.wait_ge(npre_ready, p * 2 + (h + 1))
                    act.activation(gn[:, h, :], gn[:, h, :], ACT.Tanh, bias=bih_s[:, 2:3]).then_inc(n_ready, 1)
                return step

            def gru_steps(p):
                return {3: [x1t_step(0, p)], 5: [rz_step(0, p)], 6: [x1t_step(1, p)], 7: [n_step(0, p)],
                        8: [rz_step(1, p)], 10: [n_step(1, p)]}

            def round_step(T):
                def step(u):
                    act.activation(rounded.bitcast(f32r), feat[:, bass.ds(T * NU, NU), 1, :], ACT.Copy)\
                       .then_inc(x1_rounded, 1)
                return step

            def keep_hi_step(T, n):
                def step(u):
                    wait_alone(act, x1_lo_kept, n + 1)
                    act.activation(feat[:, bass.ds(T * NU, NU), 1, :], rounded, ACT.Copy).then_inc(x1_hi_kept, 1)
                return step

            round_step(NP - 1)(None)
            keep_hi_step(NP - 1, 0)(None)
            act.wait_ge(x1_hi_kept, 1)
            split_hi(NP - 1, 3, steps={2: [keep(0, 0, NP - 1), keep(0, 1, NP - 1)], 3: [round_step(NP - 2)],
                                       6: [keep_hi_step(NP - 2, 1)]})
            act.wait_ge(feat1_ready, 2 * NP)
            with act.Fori(0, NP - 2) as k:
                wait_alone(act, x1_hi_kept, k + 2)
                split_hi(NP - 2 - k, 3, steps={3: [round_step(NP - 3 - k)], 6: [keep_hi_step(NP - 3 - k, k + 2)]})
            act.wait_ge(x1_hi_kept, NP)
            split_hi(0, 3)
            with act.Fori(0, NP - 3) as i:
                split_hi(NP - 2 - i, 3, steps=part1(gru_steps(i)))
                split_hi(NP - 3 - i, 3, steps=part2(gru_steps(i)))
                with act.Fori(i, NP - 3) as k:
                    split_hi(NP - 4 - k, 3)
            split_hi(1, 3, steps=part1(gru_steps(NP - 3)))
            split_hi(0, 3, steps=part2(gru_steps(NP - 3)))
            split_hi(0, 3, steps=part1(gru_steps(NP - 2)))
            for step in tail(part2(gru_steps(NP - 2)), gru_steps(NP - 1)):
                step(None)

        @block.vector
        def _(dve):
            chain = Chain(dve, dve_chain, "dve_chain_at")

            dve.memset(zeros[:, :], 0.0)
            dve.memset(ones[:, :], 1.0).then_inc(zeroed, 2)
            dve.memset(eps_ln[:, :, :], LN_EPS).then_inc(zeroed, 1)
            dve.wait_ge(weights_in, NW * 16)
            dve.tensor_tensor(brz[:, 0:1], bih_s[:, 0:1], bhh_s[:, 0:1], ALU.add)
            dve.scalar_tensor_tensor(brz[:, 1:2], bih_s[:, 1:2], -1.0, bhh_s[:, 1:2], ALU.mult, ALU.subtract)\
               .then_inc(zeroed, 1)

            cs = colsum[:, :, :].rearrange("p u c -> p (u c)")

            def add_up(tile, sem_done, first=False):
                t = tile.rearrange("p u c -> p (u c)")
                if first:
                    dve.tensor_copy(cs, t).then_inc(sem_done, 1)
                else:
                    dve.tensor_tensor(cs, cs, t, ALU.add).then_inc(sem_done, 1)

            dve.memset(mhalf[:, :, :], -0.5).then_inc(sum_done, NS)
            with dve.Fori(0, NP) as P:
                def ring_sum(n, s, first=False, after_diag=False):
                    dve.wait_ge(ring_in[s], n * 16 + 16)
                    if after_diag:
                        dve.wait_ge(dsum_done, P * NS + NS)
                    elif not first:
                        dve.wait_ge(sum_done, n * NS + (NS + s))
                    add_up(ring[:, s], sum_done, first=first)

                n0 = P * (NP - 1)
                for s in range(NS):
                    ring_sum(n0, s, first=s == 0)
                with dve.Fori(1, NP - 2) as k:
                    for s in range(NS):
                        ring_sum(n0 + k, s)
                for s in range(NS):
                    dve.wait_ge(diag_in[s], P * 16 + 16)
                    if s == 0:
                        dve.wait_ge(sum_done, n0 * NS + (NP - 1) * NS)
                    else:
                        dve.wait_ge(dsum_done, P * NS + s)
                    add_up(diag[:, s], dsum_done)
                for s in range(NS):
                    ring_sum(n0 + (NP - 2), s, after_diag=s == 0)
                dve.wait_ge(sum_done, P * ((NP - 1) * NS) + NP * NS)
                dve.tensor_tensor(csum[:, :], colsum[:, 0, :], colsum[:, 1, :], ALU.add).then_inc(csum_ready, 1)
                dve.wait_ge(deg_done, P + 1)
                dve.tensor_scalar(deg[:, :, 0], p_deg[:, 0:NU], DEG_EPS, None, ALU.add).then_inc(deg_ready, 1)
                wait_alone(dve, dinv_ready, P + 1)
                for h in range(2):
                    t0 = P * NU + h * NB
                    dve.tensor_tensor(feat[:, bass.ds(t0, NB), 0, :], tr[h][:, :].rearrange("p (b f) -> p b f", b=NB),
                                      dinv[:, bass.ds(t0, NB), :].to_broadcast([128, NB, D]), ALU.mult)\
                       .then_inc(feat0_ready, 1)

            units = Tally(dve, "dve_units", NU)

            def split_lo(T, sweep, first=False, steps={}):
                u = 0 if first else units.now()
                chain.begin()
                for q in range(NU):
                    dve.wait_ge(hi_ready, u + (q + 1))
                    last = dve.tensor_tensor(a_lo[:, q % 4, :], ring[:, q // 2, q % 2, :],
                                             a_hi[:, q % 4, :].bitcast(f32), ALU.subtract)
                    if sweep == 2:
                        last = dve.tensor_tensor(f_parts[:, q % 4, 0, :, :], feat[:, bass.ds(T * NU + q, 1), :, :]
                                                 .rearrange("p o l f -> p (o l) f"),
                                                 f_parts[:, q % 4, 1, :, :].bitcast(f32), ALU.subtract)
                    last.then_inc(lo_ready, 1)
                    for step in steps.get(q, ()):
                        step(u)
                chain.end()
                if not first:
                    units.add(NU)

            def norm_stats(h, rows, at):
                for b in range(NB):
                    last = dve.bn_stats(stats[:, h, b, :], rows(b))
                chain.link(last, wait_alone)
                for b in range(NB):
                    last = dve.bn_aggr(mv[:, h, b, :], stats[:, h, b, :])
                last.then_inc(var_ready, 1)

            def normalize(h, rows, to, at):
                dve.wait_ge(rstd_ready, at)
                for b in range(NB):
                    last = dve.tensor_scalar(to(b), rows(b), mv[:, h, b, 0:1], rstd[:, h, b, :],
                                             ALU.subtract, ALU.mult)
                return last

            def tall_step(P, h, p):
                def step(u):
                    wait_alone(dve, done[0][h], u)
                    dve.tensor_tensor(tall[:, h, :], part[:, bass.ds(P * W + h * HALF, HALF)], acc0[h][:, :],
                                      ALU.add).then_inc(tall_ready[h], 1)
                return step

            def rows_step(P, h, p):
                def step(u):
                    t0 = P * NU + h * NB
                    yh = y[:, h, :, :]
                    dve.wait_ge(turned[h], p + 1)
                    ins = dve.tensor_tensor(yh, feat[:, bass.ds(t0, NB), 0, :],
                                            tr[h][:, :].rearrange("p (b f) -> p b f", b=NB), ALU.add)
                    chain.link(ins)
                    ins = dve.tensor_tensor(yh, yh, dinv[:, bass.ds(t0, NB), :].to_broadcast([128, NB, D]), ALU.mult)
                    ins.then_inc(turned_used[h], 1)
                    dve.wait_ge(turned_used[h], p + 1)
                    dve.wait_ge(xin_in, p * 16 + 16)
                    chain.link(dve.tensor_tensor(yh, yh, xin[:, h * NB:(h + 1) * NB, :], ALU.add))
                    norm_stats(h, lambda b: y[:, h, b, :], None)
                return step

            def x1_step(P, h, p):
                def step(u):
                    t0 = P * NU + h * NB
                    normalize(h, lambda b: y[:, h, b, :],
                              lambda b: feat[:, bass.ds(t0 + b, 1), 1, :].rearrange("p o f -> p (o f)"),
                              p * 2 + (h + 1)).then_inc(feat1_ready, 1)
                return step

            def layer0_steps(P, p):
                return {2: [tall_step(P, 0, p), tall_step(P, 1, p)], 4: [rows_step(P, 0, p)],
                        5: [rows_step(P, 1, p), x1_step(P, 0, p)], 6: [x1_step(P, 1, p)]}

            dve.wait_ge(feat0_ready, 2 * NP)
            chain.begin()
            for h in range(2):
                dve.wait_ge(part_ready, 2 * NP)
                cols = slice((NP - 1) * W + h * HALF, (NP - 1) * W + (h + 1) * HALF)
                ins = dve.tensor_copy(tall[:, h, :], part[:, cols])
                ins.then_inc(tall_ready[h], 1)
                dve.wait_ge(tall_ready[h], 1)
                chain.link(dve.memset(part[:, cols], 0.0))
            for h in range(2):
                rows_step(NP - 1, h, 0)(0)
                x1_step(NP - 1, h, 0)(0)
            chain.end()
            dve.wait_ge(feat1_ready, 2)
            split_lo(NP - 1, 2, first=True)
            with dve.Fori(0, NP - 2) as i:
                split_lo(NP - 1, 2, steps=layer0_steps(NP - 2 - i, i + 1))
                wait_alone(dve, feat1_ready, i * 2 + 4)
                with dve.Fori(0, i + 1) as k:
                    split_lo(NP - 2 - k, 2)

            def agg_step(P, h, p):
                def step(u):
                    wait_alone(dve, done[1][h], u)
                    dve.tensor_tensor(tall[:, h, :], part[:, bass.ds(P * W + h * HALF, HALF)], acc1[h][:, :],
                                      ALU.add).then_inc(agg_ready[h], 1)
                return step

            def npre_step(h, p):
                def step(u):
                    n = gn[:, h, :]
                    dve.wait_ge(rz_ready, p * 2 + (h + 1))
                    chain.link(dve.scalar_tensor_tensor(n, p_hn[:, :], bhh_s[:, 2:3], gr[:, h, :], ALU.add, ALU.mult))
                    dve.tensor_tensor(n, n, p_in[:, :], ALU.add).then_inc(npre_ready, 1)
                return step

            def sum_step(h, p):
                def step(u):
                    t = tall[:, h, :]
                    dve.wait_ge(x1t_ready, p * 2 + (h + 1))
                    dve.wait_ge(n_ready, p * 2 + (h + 1))
                    chain.link(dve.tensor_tensor(t, x1t[:, h, :], gn[:, h, :], ALU.subtract))
                    chain.link(dve.tensor_tensor(t, t, gz[:, h, :], ALU.mult))
                    dve.scalar_tensor_tensor(t, x1t[:, h, :], 2.0, t, ALU.mult, ALU.subtract).then_inc(sum_ready, 1)
                return step

            def out_step(h, p):
                def step(u):
                    rows = lambda b: p_tr[:, b * 128:(b + 1) * 128]
                    dve.wait_ge(rows_done, p * 2 + (h + 1))
                    norm_stats(h, rows, None)
                    normalize(h, rows, lambda b: y[:, h, b, :], p * 2 + (2 * NP + h + 1)).then_inc(rows_used, 1)
                return step

            def gru_steps(P, p):
                return {1: [agg_step(P, 0, p), agg_step(P, 1, p)], 5: [npre_step(0, p)], 7: [sum_step(0, p)],
                        8: [npre_step(1, p)], 10: [sum_step(1, p)], 11: [out_step(0, p)], 14: [out_step(1, p)]}

            def keep_lo_step(T, n):
                def step(u):
                    wait_alone(dve, x1_rounded, n + 1)
                    dve.tensor_tensor(feat[:, bass.ds(T * NU, NU), 0, :], feat[:, bass.ds(T * NU, NU), 1, :],
                                      rounded, ALU.subtract).then_inc(x1_lo_kept, 1)
                return step

            keep_lo_step(NP - 1, 0)(None)
            steps = layer0_steps(0, NP - 1)
            steps[4] = [keep_lo_step(NP - 2, 1)] + steps[4]
            split_lo(NP - 1, 3, steps=steps)
            dve.wait_ge(feat1_ready, 2 * NP)
            with dve.Fori(0, NP - 2) as k:
                split_lo(NP - 2 - k, 3, steps={4: [keep_lo_step(NP - 3 - k, k + 2)]})
            split_lo(0, 3)
            with dve.Fori(0, NP - 3) as i:
                split_lo(NP - 2 - i, 3, steps=part1(gru_steps(NP - 1 - i, i)))
                split_lo(NP - 3 - i, 3, steps=part2(gru_steps(NP - 1 - i, i)))
                with dve.Fori(i, NP - 3) as k:
                    split_lo(NP - 4 - k, 3)
            split_lo(1, 3, steps=part1(gru_steps(2, NP - 3)))
            split_lo(0, 3, steps=part2(gru_steps(2, NP - 3)))
            split_lo(0, 3, steps=part1(gru_steps(1, NP - 2)))
            u = units.now()
            chain.begin()
            for step in tail(part2(gru_steps(1, NP - 2)), gru_steps(0, NP - 1)):
                step(u)
            chain.end()

        @block.gpsimd
        def _(pool):
            pool.memset(ident[:, :], 0.0).then_inc(consts, 0 + 1)
            pool.wait_ge(consts, 1)
            pool.affine_select(out=ident[:, :], in_=ident[:, :], compare_op=ALU.not_equal, fill=1.0,
                               base=0, pattern=[[-1, 128]], channel_multiplier=1).then_inc(consts, 1)
            pool.wait_ge(zeroed, 4)
            pool.wait_ge(sum_done, NS)

            def load_xt(P):
                pool.dma_start(xt[:, :], x_t[:, bass.ds(P * W, W)]).then_inc(xt_in, 16)

            def degrees(P):
                pool.wait_ge(deg_ready, P + 1)
                pool.tensor_tensor(dinv[:, bass.ds(P * NU, NU), :], deg[:, :, :], mhalf[:, :, :], ALU.pow)\
                    .then_inc(dinv_ready, 1)

            load_xt(0)
            with pool.Fori(0, NP - 1) as P:
                pool.wait_ge(supp_done, P + 1)
                load_xt(P + 1)
                degrees(P)
            degrees(NP - 1)

            def deviation(h, at):
                pool.wait_ge(var_ready, at)
                pool.tensor_tensor(var[:, h, :, :], mv[:, h, :, 1:2], eps_ln[:, 0:NB, :], ALU.add).then_inc(veps_ready, 1)
                pool.wait_ge(veps_ready, at)
                pool.tensor_tensor(rstd[:, h, :, :], var[:, h, :, :], mhalf[:, 0:NB, :], ALU.pow).then_inc(rstd_ready, 1)

            with pool.Fori(0, NP) as p:
                pool.dma_start(xin[:, :, :], x_rows[:, bass.ds((NP - 1 - p) * NU, NU), :]).then_inc(xin_in, 16)
                for h in range(2):
                    deviation(h, p * 2 + (h + 1))
            pool.wait_ge(x1_hi_kept, NP)
            with pool.Fori(0, NP) as p:
                for h in range(2):
                    t0 = (NP - 1 - p) * NU + h * NB
                    pool.tensor_tensor(xin[:, h * NB:(h + 1) * NB, :], feat[:, bass.ds(t0, NB), 0, :],
                                       feat[:, bass.ds(t0, NB), 1, :], ALU.add).then_inc(x1_ready, 1)
                for h in range(2):
                    deviation(h, p * 2 + (2 * NP + h + 1))
                    pool.wait_ge(rows_used, p * 2 + (h + 1))
                    pool.dma_start(out_rows[:, bass.ds((NP - 1 - p) * NU + h * NB, NB), :], y[:, h, :, :])\
                        .then_inc(stored[h], 16)
                for h in range(2):
                    wait_alone(pool, stored[h], p * 16 + 16)


def kernel(x, adj, L0_gnn_weight, L1_gnn_W_msg, L1_gnn_b_msg, L1_gnn_W_ih, L1_gnn_W_hh, L1_gnn_b_ih, L1_gnn_b_hh):
    import numpy as np
    import concourse.bacc as bacc
    from concourse.bass_utils import run_bass_kernel_spmd

    W, NP, D = 1024, 8, 128
    a = np.asarray(adj).reshape(NP, W, NP, 4, 2, 128).transpose(0, 2, 3, 5, 4, 1)
    blocks = np.empty((NP * NP, 4, 128, 2, W), a.dtype)
    for P in range(NP):
        for k in range(NP):
            blocks[P * NP + k] = a[P, (P - k) % NP]
    c = np.ascontiguousarray
    arrays = {
        "adj_blocks": blocks,
        "x_t": c(np.asarray(x).T),
        "x": c(np.asarray(x)),
        "w0": c(np.asarray(L0_gnn_weight)),
        "wmsg_t": c(np.asarray(L1_gnn_W_msg).T),
        "b_msg": c(np.asarray(L1_gnn_b_msg).reshape(1, D).T),
        "wih_t": c(np.asarray(L1_gnn_W_ih).T),
        "whh_t": c(np.asarray(L1_gnn_W_hh).T),
        "b_ih": c(np.asarray(L1_gnn_b_ih).reshape(3, D).T),
        "b_hh": c(np.asarray(L1_gnn_b_hh).reshape(3, D).T),
    }
    nc = bacc.Bacc("TRN2", target_bir_lowering=False, num_devices=1)
    aps = {n: nc.dram_tensor(n, v.shape, mybir.dt.from_np(v.dtype), kind="ExternalInput").ap()
           for n, v in arrays.items()}
    out = nc.dram_tensor("out", (NP * W, D), mybir.dt.float32, kind="ExternalOutput").ap()
    gnn_resnorm_kernel(nc, **aps, out=out)
    return run_bass_kernel_spmd(nc, [arrays], core_ids=[0]).results[0]["out"]
```

```python
import concourse.bass as bass
from concourse import mybir
from contextlib import ExitStack



class Tally:

    def __init__(self, eng, name, start=0):
        self.eng = eng
        self.reg = eng.alloc_register(name)
        eng.reg_mov(self.reg, start)

    def now(self):
        return self.eng.snap(self.reg)

    def add(self, n):
        self.eng.reg_add(self.reg, self.reg, n)


class Chain:

    def __init__(self, eng, sem, name):
        self.eng, self.sem, self.tally, self.k, self.base = eng, sem, Tally(eng, name), 0, None

    def begin(self):
        self.k, self.base = 0, self.tally.now()

    def link(self, ins, wait=None):
        ins.then_inc(self.sem, 1)
        self.k += 1
        if wait:
            wait(self.eng, self.sem, self.base + self.k)
        else:
            self.eng.wait_ge(self.sem, self.base + self.k)

    def end(self):
        self.tally.add(self.k)


def gnn_resnorm_kernel(nc, adj_blocks, x_t, x, w0, wmsg_t, b_msg, wih_t, whh_t, b_ih, b_hh, out):
    f32, f32r = mybir.dt.float32, mybir.dt.float32r
    ALU, ACT = mybir.AluOpType, mybir.ActivationFunctionType

    D = 128
    N = x.shape[0]
    W = 1024
    NP = N // W
    NU = W // 128
    NS = NU // 2
    HALF = 512
    NB = HALF // 128
    RING1 = NP * (NP - 1)
    PROD1 = NP * (NP + 1) // 2
    LN_EPS, DEG_EPS = 1e-5, 1e-6
    BIAS = NU

    x_rows = x.rearrange("(t p) f -> p t f", p=128)
    out_rows = out.rearrange("(t p) f -> p t f", p=128)

    ctx = ExitStack()
    with ctx:
        def sb(name, shape, dt=f32, at=ctx):
            return at.enter_context(nc.sbuf_tensor(name, shape, dt))

        def sem(name):
            return ctx.enter_context(nc.semaphore(name))

        feat = sb("feat", [128, N // 128, 2, D])
        part = sb("part", [128, N])
        ring = sb("ring", [128, NS, 2, W])
        tall = sb("tall", [128, 2, HALF])
        y = sb("y", [128, 2, NB, D])
        xin = sb("xin", [128, NU, D])
        stats = sb("stats", [128, 2, NB, 6])
        mv = sb("mv", [128, 2, NB, 2])
        var = sb("var", [128, 2, NB, 1])
        rstd = sb("rstd", [128, 2, NB, 1])
        deg = sb("deg", [128, NU, 1])
        dinv = sb("dinv", [128, N // 128, 1])
        mhalf = sb("mhalf", [128, NU, 1])
        ones = sb("ones", [128, 1])
        zeros = sb("zeros", [1, HALF], mybir.dt.bfloat16)
        ident = sb("ident", [128, 128])
        w0_s = sb("w0_s", [128, D])
        wmsg_s = sb("wmsg_s", [128, D])
        wih_s = sb("wih_s", [128, 3 * D])
        whh_s = sb("whh_s", [128, 3 * D])
        bmsg_s = sb("bmsg_s", [128, 1])
        bih_s = sb("bih_s", [128, 3])
        bhh_s = sb("bhh_s", [128, 3])
        brz = sb("brz", [128, 2])
        weights = [(w0_s[:, :], w0), (wmsg_s[:, :], wmsg_t), (wih_s[:, :], wih_t), (whh_s[:, :], whh_t),
                   (bmsg_s[:, :], b_msg), (bih_s[:, :], b_ih), (bhh_s[:, :], b_hh)]
        NW = len(weights)
        eps_ln = sb("eps_ln", [128, NU, 1])
        with ExitStack() as early:
            diag = sb("diag", [128, NS, 2, W], at=early)
            colsum = sb("colsum", [128, 2, W], at=early)
            csum = sb("csum", [128, W], at=early)
            xt = sb("xt", [128, 2, W], at=early)
            feat_stage = sb("feat_stage", [128, 4, D], at=early)
        a_hi = sb("a_hi", [128, 4, W], f32r)
        a_lo = sb("a_lo", [128, 4, W], f32r)
        f_parts = sb("f_parts", [128, 4, 2, 2, D], f32r)
        x1t = sb("x1t", [128, 2, HALF])
        rounded = x1t[:, :, :].rearrange("p h c -> p (h c)").rearrange("p (t f) -> p t f", f=D)
        msgt = sb("msgt", [128, 2, HALF])
        gr = sb("gr", [128, 2, HALF])
        gz = sb("gz", [128, 2, HALF])
        gn = sb("gn", [128, 2, HALF])

        bank = [ctx.enter_context(nc.psum_tensor(f"bank{i}", [128, HALF], f32)) for i in range(8)]
        acc0, acc1 = bank[0:2], bank[2:4]
        tr = bank[4:6]
        supp = tr, acc1
        p_deg = bank[6]
        p_msg, p_tr, p_r, p_z, p_in, p_hn = bank[4], bank[5], bank[0], bank[1], bank[6], bank[7]
        p_rows = p_tr, p_msg

        ring_in = [sem(f"ring_in{s}") for s in range(NS)]
        diag_in = [sem(f"diag_in{s}") for s in range(NS)]
        xt_in = [sem(f"xt_in{s}") for s in range(2)]
        xin_in, weights_in = sem("xin_in"), sem("weights_in")
        stored = [sem(f"stored{h}") for h in range(2)]
        zeroed, consts = sem("zeroed"), sem("consts")
        sum_done = sem("sum_done")
        dsum_done = sem("dsum_done")
        csum_ready = sem("csum_ready")
        supp_done = sem("supp_done")
        supp_ready = sem("supp_ready")
        deg_done = sem("deg_done")
        deg_ready = sem("deg_ready")
        dinv_ready = sem("dinv_ready")
        feat0_ready = sem("feat0_ready")
        staged = sem("staged")
        prod_done = sem("prod_done")
        part_ready = sem("part_ready")
        hi_ready, lo_ready = sem("hi_ready"), sem("lo_ready")
        done = [[sem(f"done{l}{h}") for h in range(2)] for l in range(2)]
        tall_ready = [sem(f"tall_ready{h}") for h in range(2)]
        kept = [sem(f"kept{h}") for h in range(2)]
        turned = [sem(f"turned{h}") for h in range(2)]
        turned_used = [sem(f"turned_used{h}") for h in range(2)]
        xin_used = sem("xin_used")
        var_ready, veps_ready, rstd_ready = sem("var_ready"), sem("veps_ready"), sem("rstd_ready")
        feat1_ready = sem("feat1_ready")
        x1_rounded, x1_lo_kept, x1_hi_kept = sem("x1_rounded"), sem("x1_lo_kept"), sem("x1_hi_kept")
        agg_ready = [sem(f"agg_ready{h}") for h in range(2)]
        x1_ready, x1t_done, x1t_ready = sem("x1_ready"), sem("x1t_done"), sem("x1t_ready")
        msg_done, msg_ready = sem("msg_done"), sem("msg_ready")
        gates_done, rz_ready = sem("gates_done"), sem("rz_ready")
        npre_ready, n_ready = sem("npre_ready"), sem("n_ready")
        sum_ready, rows_done, rows_used = sem("sum_ready"), sem("rows_done"), sem("rows_used")
        y_ready = sem("y_ready")
        dve_chain = sem("dve_chain")
        passed = sem("passed")

        def wait_alone(eng, sem, value):
            eng.wait_ge(sem, value)
            eng.sem_inc(passed, 1)

        def part1(steps):
            return {q: s for q, s in steps.items() if q < NU}

        def part2(steps):
            return {q - NU: s for q, s in steps.items() if q >= NU}

        def tail(*epilogues):
            return [step for steps in epilogues for q in sorted(steps) for step in steps[q]]

        block = ctx.enter_context(nc.Block())

        @block.sync
        def _(sp):
            before = Tally(sp, "sp_before")

            def load(s, blk):
                sp.dma_start(ring[:, s], adj_blocks[bass.ds(blk, 1), s].rearrange("o p u c -> (o p) u c"))\
                  .then_inc(ring_in[s], 16)

            def ring_load1(n, at, products):
                for s in range(NS):
                    wait_alone(sp, sum_done, n * NS + (s + 1))
                    if products is not None:
                        wait_alone(sp, prod_done, products * NU + (2 * s + 2))
                    load(s, at)

            def load_diag(P, b):
                for s in range(NS):
                    if b is not None:
                        wait_alone(sp, prod_done, b * NU + (2 * s + 2 + NU))
                    sp.dma_start(diag[:, s], adj_blocks[bass.ds(P * NP, 1), s]
                                 .rearrange("o p u c -> (o p) u c")).then_inc(diag_in[s], 16)

            def upper(P, b):
                with sp.Fori(0, NP - 1 - P) as k:
                    ring_load1(P * (NP - 1) + k, P * NP + (NP - 1 - k), b)

            def lower(P, first, b):
                ring_load1(P * (NP - 2) + (NP - 1), P * (NP + 1), b)
                load_diag(P, b)
                if not first:
                    with sp.Fori(1, P) as t:
                        ring_load1(P * (NP - 2) + (t + (NP - 1)), P * (NP + 1) - t, b + (t + 1))
                before.add(P + 1)

            upper(0, None)
            load_diag(0, None)
            b = before.now()
            upper(1, b)
            lower(1, True, b)
            with sp.Fori(2, NP - 1) as P:
                b = before.now()
                upper(P, b)
                lower(P, False, b)
            lower(NP - 1, False, before.now())

            units = Tally(sp, "sp_units", NU)

            def ring_load(blk, first=False):
                u = 0 if first else units.now()
                for s in range(NS):
                    if first:
                        sp.wait_ge(sum_done, RING1 * NS + s + 1)
                        sp.wait_ge(prod_done, (PROD1 - 1) * NU + 2 * s + 2)
                    else:
                        wait_alone(sp, lo_ready, u + (2 * s + 2 - NU))
                    load(s, blk)
                if not first:
                    units.add(NU)

            ring_load((NP - 2) * NP + NP - 1, first=True)
            with sp.Fori(0, NP - 2) as i:
                with sp.Fori(NP - 2 - i, NP) as k:
                    ring_load((NP - 3 - i) * NP + k)
            with sp.Fori(0, NP) as k:
                ring_load((NP - 1) * NP + k)
            ring_load(0)
            with sp.Fori(1, NP - 1) as i:
                with sp.Fori(0, NP - i) as k:
                    ring_load((NP - 1 - i) * NP + k)

        @block.tensor
        def _(pe):
            blocks1 = Tally(pe, "pe_blocks1")

            def product1(c, src, ready, value, steps={}):
                for q in range(NU):
                    if q % 2 == 0:
                        pe.wait_ge(ready[q // 2], value)
                    pe.wait_ge(staged, c * NU + (q + 1))
                    for h in range(2):
                        mm = pe.matmul(acc0[h][:, :], feat_stage[:, q % 4, :],
                                       src[:, q // 2, q % 2, h * HALF:(h + 1) * HALF],
                                       start=False, stop=True, skip_group_check=True)
                    mm.then_inc(prod_done, 1)
                    for step in steps.get(q, ()):
                        step()

            def panel1(P, lower):
                def degrees():
                    pe.wait_ge(csum_ready, P + 1)
                    for b in range(NU):
                        mm = pe.matmul(p_deg[:, b:b + 1], csum[:, b * 128:(b + 1) * 128], ones[:, :],
                                       start=True, stop=True)
                    mm.then_inc(deg_done, 1)

                def ring_product(t, steps={}):
                    product1(c + t, ring, ring_in, (P * (NP - 2) + (NP + t)) * 16, steps)

                c = blocks1.now()
                if lower:
                    pe.wait_ge(part_ready, P * 2)
                for h in range(2):
                    pe.matmul(acc0[h][:, :], zeros[0:1, 0:128], zeros[0:1, :], start=True, stop=True)
                if lower > 1:
                    with pe.Fori(0, P - 1) as t:
                        ring_product(t)
                    ring_product(P - 1, {NU - 2: [degrees]})
                else:
                    if lower:
                        ring_product(0)
                    degrees()
                product1(c + P, diag, diag_in, P * 16 + 16)
                blocks1.add(P + 1)

            pe.wait_ge(consts, 2)
            pe.wait_ge(zeroed, 4)
            pe.wait_ge(weights_in, NW * 16)
            pe.matmul(acc0[0][:, 0:128], zeros[0:1, 0:128], zeros[0:1, 0:128], start=True, stop=True)\
              .then_inc(prod_done, BIAS)

            def support(P, s, first=False):
                pe.wait_ge(xt_in[s], P * 8 + (16 - 8 * s))
                if not first:
                    pe.wait_ge(supp_ready, P - 1)
                for b in range(NU):
                    mm = pe.matmul(supp[s][b // NB][:, (b % NB) * D:(b % NB + 1) * D],
                                   xt[:, s, b * 128:(b + 1) * 128], w0_s[:, :], start=True, stop=True)
                mm.then_inc(supp_done, 1)

            support(0, 0, True)
            support(1, 1, True)
            with pe.Fori(1, NP // 2) as i:
                support(i * 2, 0)
                support(i * 2 + 1, 1)

            panel1(0, 0)
            panel1(1, 1)
            with pe.Fori(2, NP) as P:
                panel1(P, 2)

            units = Tally(pe, "pe_units")

            def multiply(layers, begin, freed=None, steps={}):
                u = units.now()
                for q in range(NU):
                    pe.wait_ge(lo_ready, u + (q + 1))
                    for l in layers:
                        for h in range(2):
                            first = begin and q == 0
                            if first and freed:
                                freed(l, h)
                            cols = slice(h * HALF, (h + 1) * HALF)
                            acc = (acc0, acc1)[l][h][:, :]
                            pe.matmul(acc, f_parts[:, q % 4, 1, l, :], a_hi[:, q % 4, cols],
                                      start=first, stop=False, skip_group_check=True)
                            pe.matmul(acc, f_parts[:, q % 4, 1, l, :], a_lo[:, q % 4, cols],
                                      start=False, stop=False, skip_group_check=True)
                            pe.matmul(acc, f_parts[:, q % 4, 0, l, :], a_hi[:, q % 4, cols],
                                      start=False, stop=True, skip_group_check=True).then_inc(done[l][h], 1)
                    for step in steps.get(q, ()):
                        step()
                units.add(NU)

            def turn(h, p):
                pe.wait_ge(tall_ready[h], p + 1)
                if not isinstance(p, int) or p:
                    pe.wait_ge(turned_used[h], p)
                for b in range(NB):
                    t = pe.transpose(tr[h][:, b * 128:(b + 1) * 128], tall[:, h, b * 128:(b + 1) * 128], ident[:, :])
                t.then_inc(turned[h], 1)

            pe.wait_ge(feat0_ready, 2 * NP)
            turn(0, 0)
            turn(1, 0)
            pe.wait_ge(part_ready, 2 * NP)
            multiply((0, 1), True)
            with pe.Fori(0, NP - 2) as i:
                def freed2(l, h):
                    if l == 0:
                        pe.wait_ge(tall_ready[h], i + 2)
                    else:
                        pe.wait_ge(kept[h], i + 1)

                multiply((0, 1), True, freed2, {0: [lambda: turn(0, i + 1), lambda: turn(1, i + 1)]})
                with pe.Fori(0, i + 1) as k:
                    multiply((0, 1), False)

            def x1_step(h, p):
                pe.wait_ge(x1_ready, p * 2 + (h + 1))
                if h == 1:
                    pe.wait_ge(x1t_ready, p * 2 + 1)
                for b in range(NB):
                    t = pe.transpose(p_tr[:, b * 128:(b + 1) * 128], xin[:, h * NB + b, :], ident[:, :])
                t.then_inc(x1t_done, 1)

            def msg_step(P, h, p):
                wait_alone(pe, agg_ready[h], p + 1)
                pe.matmul(p_msg[:, :], wmsg_s[:, :], part[:, bass.ds(P * W + h * HALF, HALF)], start=True, stop=True)\
                  .then_inc(msg_done, 1)

            def gates_step(h, p):
                pe.wait_ge(msg_ready, p * 2 + (h + 1))
                pe.wait_ge(x1t_ready, p * 2 + (h + 1))
                if h == 1:
                    pe.wait_ge(npre_ready, p * 2 + 1)
                m, s = msgt[:, h, :], x1t[:, h, :]
                for g, bank_g in ((0, p_r), (1, p_z)):
                    pe.matmul(bank_g[:, :], wih_s[:, g * D:(g + 1) * D], m, start=True, stop=False)
                    pe.matmul(bank_g[:, :], whh_s[:, g * D:(g + 1) * D], s, start=False, stop=True)
                pe.matmul(p_in[:, :], wih_s[:, 2 * D:3 * D], m, start=True, stop=True)
                pe.matmul(p_hn[:, :], whh_s[:, 2 * D:3 * D], s, start=True, stop=True).then_inc(gates_done, 1)

            def rows_step(h, p):
                pe.wait_ge(sum_ready, p * 2 + (h + 1))
                pe.wait_ge((x1t_ready, msg_ready)[h], p * 2 + 2)
                for b in range(NB):
                    t = pe.transpose(p_rows[h][:, b * 128:(b + 1) * 128], tall[:, h, b * 128:(b + 1) * 128], ident[:, :])
                t.then_inc(rows_done, 1)

            def gru_steps(P, p):
                return {0: [lambda: x1_step(0, p), lambda: msg_step(P, 0, p)],
                        2: [lambda: gates_step(0, p), lambda: x1_step(1, p), lambda: msg_step(P, 1, p)],
                        4: [lambda: gates_step(1, p)], 8: [lambda: rows_step(0, p)], 11: [lambda: rows_step(1, p)]}

            def freed3(p):
                return lambda l, h: pe.wait_ge(agg_ready[h], p + 1)

            multiply((1,), True, lambda l, h: pe.wait_ge(kept[h], NP - 1),
                     {0: [lambda: turn(0, NP - 1)], 1: [lambda: turn(1, NP - 1)]})
            with pe.Fori(0, NP - 1) as k:
                multiply((1,), False)
            for h in range(2):
                pe.wait_ge(turned_used[h], NP)
            multiply((1,), True, freed3(0), part1(gru_steps(NP - 1, 0)))
            multiply((1,), True, freed3(1), part2(gru_steps(NP - 1, 0)))
            multiply((1,), False, None, part1(gru_steps(0, 1)))
            multiply((1,), False, None, part2(gru_steps(0, 1)))
            with pe.Fori(0, NP - 4) as k:
                multiply((1,), False)
            with pe.Fori(0, NP - 4) as i:
                steps = gru_steps(NP - 2 - i, i + 2)
                multiply((1,), True, freed3(i + 2), part1(steps))
                multiply((1,), False, None, part2(steps))
                with pe.Fori(0, NP - 4 - i) as k:
                    multiply((1,), False)
            multiply((1,), True, freed3(NP - 2), part1(gru_steps(2, NP - 2)))
            multiply((1,), False, None, part2(gru_steps(2, NP - 2)))
            for step in tail(gru_steps(1, NP - 1)):
                step()

        @block.scalar
        def _(act):
            blocks1 = Tally(act, "act_blocks1")

            for dst, src in weights:
                act.dma_start(dst, src).then_inc(weights_in, 16)

            def stage1(c, T):
                for q in range(NU):
                    act.wait_ge(prod_done, c * NU + (q - 4 + 1 + BIAS))
                    act.activation(feat_stage[:, q % 4, :], feat[:, bass.ds(T * NU + q, 1), 0, :]
                                   .rearrange("p o f -> p (o f)"), ACT.Copy).then_inc(staged, 1)

            def panel1(P, lower):
                c = blocks1.now()
                if lower:
                    act.wait_ge(feat0_ready, P * 2)
                    with act.Fori(0, P) as t:
                        stage1(c + t, t)
                act.wait_ge(feat0_ready, P * 2 + 2)
                stage1(c + P, P)
                act.wait_ge(prod_done, (c + P) * NU + (NU + BIAS))
                for h in range(2):
                    act.activation(part[:, bass.ds(P * W + h * HALF, HALF)], acc0[h][:, :], ACT.Copy)\
                       .then_inc(part_ready, 1)
                blocks1.add(P + 1)

            with act.Fori(0, NP // 2) as i:
                for s in range(2):
                    act.wait_ge(supp_done, i * 2 + (s + 1))
                    for h in range(2):
                        ins = act.activation(feat[:, bass.ds(i * (2 * NU) + (s * NU + h * NB), NB), 1, :],
                                             supp[s][h][:, :].rearrange("p (b f) -> p b f", b=NB), ACT.Copy)
                    ins.then_inc(supp_ready, 1)

            panel1(0, False)
            with act.Fori(1, NP) as P:
                panel1(P, True)

            units = Tally(act, "act_units", NU)

            def split_hi(T, sweep, first=False, steps={}):
                u = 0 if first else units.now()
                for q in range(NU):
                    if q % 2 == 0:
                        act.wait_ge(ring_in[q // 2], u * 2 + (RING1 + 1) * 16)
                    if q >= 4 or not first:
                        act.wait_ge(done[1][1], u + (q - 4 + 1))
                    act.activation(a_hi[:, q % 4, :], ring[:, q // 2, q % 2, :], ACT.Copy)
                    to = f_parts[:, q % 4, 1, :, :] if sweep == 2 else f_parts[:, q % 4, :, 1, :]
                    act.activation(to, feat[:, bass.ds(T * NU + q, 1), :, :]
                                   .rearrange("p o l f -> p (o l) f"), ACT.Copy).then_inc(hi_ready, 1)
                    for step in steps.get(q, ()):
                        step(u)
                if not first:
                    units.add(NU)

            def keep(P, h, p):
                def step(u):
                    act.wait_ge(done[1][h], u)
                    act.wait_ge(tall_ready[h], p + 1)
                    act.activation(part[:, bass.ds(P * W + h * HALF, HALF)], acc1[h][:, :], ACT.Copy)\
                       .then_inc(kept[h], 1)
                return step

            act.wait_ge(prod_done, PROD1 * NU + BIAS)
            act.wait_ge(feat1_ready, 1)
            split_hi(NP - 1, 2, first=True, steps={NB - 1: [lambda u: act.wait_ge(feat1_ready, 2)]})
            with act.Fori(0, NP - 2) as i:
                split_hi(NP - 1, 2, steps={2: [keep(NP - 2 - i, 0, i + 1), keep(NP - 2 - i, 1, i + 1)]})
                act.wait_ge(feat1_ready, i * 2 + 4)
                with act.Fori(0, i + 1) as k:
                    split_hi(NP - 2 - k, 2)

            def x1t_step(h, p):
                def step(u):
                    act.wait_ge(x1t_done, p * 2 + (h + 1))
                    act.activation(x1t[:, h, :], p_tr[:, :], ACT.Copy).then_inc(x1t_ready, 1)
                    act.wait_ge(msg_done, p * 2 + (h + 1))
                    act.activation(msgt[:, h, :], p_msg[:, :], ACT.Relu, bias=bmsg_s[:, 0:1]).then_inc(msg_ready, 1)
                return step

            def rz_step(h, p):
                def step(u):
                    act.wait_ge(gates_done, p * 2 + (h + 1))
                    act.activation(gr[:, h, :], p_r[:, :], ACT.Sigmoid, bias=brz[:, 0:1])
                    act.activation(gz[:, h, :], p_z[:, :], ACT.Sigmoid, bias=brz[:, 1:2], scale=-1.0)\
                       .then_inc(rz_ready, 1)
                return step

            def n_step(h, p):
                def step(u):
                    act.wait_ge(npre_ready, p * 2 + (h + 1))
                    act.activation(gn[:, h, :], gn[:, h, :], ACT.Tanh, bias=bih_s[:, 2:3]).then_inc(n_ready, 1)
                return step

            def gru_steps(p):
                return {3: [x1t_step(0, p)], 5: [rz_step(0, p)], 6: [x1t_step(1, p)], 7: [n_step(0, p)],
                        8: [rz_step(1, p)], 10: [n_step(1, p)]}

            def round_step(T):
                def step(u):
                    act.activation(rounded.bitcast(f32r), feat[:, bass.ds(T * NU, NU), 1, :], ACT.Copy)\
                       .then_inc(x1_rounded, 1)
                return step

            def keep_hi_step(T, n):
                def step(u):
                    wait_alone(act, x1_lo_kept, n + 1)
                    act.activation(feat[:, bass.ds(T * NU, NU), 1, :], rounded, ACT.Copy).then_inc(x1_hi_kept, 1)
                return step

            round_step(NP - 1)(None)
            keep_hi_step(NP - 1, 0)(None)
            act.wait_ge(x1_hi_kept, 1)
            split_hi(NP - 1, 3, steps={2: [keep(0, 0, NP - 1), keep(0, 1, NP - 1)], 3: [round_step(NP - 2)],
                                       6: [keep_hi_step(NP - 2, 1)]})
            act.wait_ge(feat1_ready, 2 * NP)
            with act.Fori(0, NP - 2) as k:
                wait_alone(act, x1_hi_kept, k + 2)
                split_hi(NP - 2 - k, 3, steps={3: [round_step(NP - 3 - k)], 6: [keep_hi_step(NP - 3 - k, k + 2)]})
            act.wait_ge(x1_hi_kept, NP)
            split_hi(0, 3)
            split_hi(0, 3, steps=part1(gru_steps(0)))
            split_hi(NP - 2, 3, steps=part2(gru_steps(0)))
            split_hi(NP - 3, 3, steps=part1(gru_steps(1)))
            split_hi(NP - 4, 3, steps=part2(gru_steps(1)))
            with act.Fori(0, NP - 4) as k:
                split_hi(NP - 5 - k, 3)
            with act.Fori(0, NP - 4) as i:
                split_hi(NP - 3 - i, 3, steps=part1(gru_steps(i + 2)))
                split_hi(NP - 4 - i, 3, steps=part2(gru_steps(i + 2)))
                with act.Fori(i, NP - 4) as k:
                    split_hi(NP - 5 - k, 3)
            split_hi(1, 3, steps=part1(gru_steps(NP - 2)))
            split_hi(0, 3, steps=part2(gru_steps(NP - 2)))
            for step in tail(gru_steps(NP - 1)):
                step(None)

        @block.vector
        def _(dve):
            chain = Chain(dve, dve_chain, "dve_chain_at")

            dve.memset(zeros[:, :], 0.0)
            dve.memset(ones[:, :], 1.0).then_inc(zeroed, 2)
            dve.memset(eps_ln[:, :, :], LN_EPS).then_inc(zeroed, 1)
            dve.wait_ge(weights_in, NW * 16)
            dve.tensor_tensor(brz[:, 0:1], bih_s[:, 0:1], bhh_s[:, 0:1], ALU.add)
            dve.scalar_tensor_tensor(brz[:, 1:2], bih_s[:, 1:2], -1.0, bhh_s[:, 1:2], ALU.mult, ALU.subtract)\
               .then_inc(zeroed, 1)

            cs = colsum[:, :, :].rearrange("p u c -> p (u c)")

            def add_up(tile, sem_done, first=False):
                t = tile.rearrange("p u c -> p (u c)")
                if first:
                    dve.tensor_copy(cs, t).then_inc(sem_done, 1)
                else:
                    dve.tensor_tensor(cs, cs, t, ALU.add).then_inc(sem_done, 1)

            dve.memset(mhalf[:, :, :], -0.5).then_inc(sum_done, NS)

            def ring_sum(n, s, first=False):
                dve.wait_ge(ring_in[s], n * 16 + 16)
                if not first:
                    dve.wait_ge(sum_done, n * NS + (NS + s))
                add_up(ring[:, s], sum_done, first=first)

            def sums(n, blocks, diag_sums=None):
                with dve.Fori(0, blocks) as k:
                    if diag_sums is not None:
                        dve.wait_ge(dsum_done, diag_sums)
                    for s in range(NS):
                        ring_sum(n + k, s)

            def diag_sums(P, value):
                for s in range(NS):
                    dve.wait_ge(diag_in[s], P * 16 + 16)
                    if s == 0:
                        dve.wait_ge(sum_done, value)
                    else:
                        dve.wait_ge(dsum_done, P * NS + s)
                    add_up(diag[:, s], dsum_done)

            def start_sums(P):
                for s in range(2, NS):
                    ring_sum(P * (NP - 1), s)

            def end_sums(P, last=False):
                dve.wait_ge(sum_done, P * ((NP - 1) * NS) + NP * NS)
                dve.wait_ge(dsum_done, P * NS + NS)
                dve.tensor_tensor(csum[:, :], colsum[:, 0, :], colsum[:, 1, :], ALU.add).then_inc(csum_ready, 1)
                if not last:
                    dve.wait_ge(csum_ready, P + 1)
                    ring_sum(P * (NP - 1) + (NP - 1), 0, first=True)
                dve.wait_ge(deg_done, P + 1)
                dve.tensor_scalar(deg[:, :, 0], p_deg[:, 0:NU], DEG_EPS, None, ALU.add).then_inc(deg_ready, 1)
                if not last:
                    ring_sum(P * (NP - 1) + (NP - 1), 1)
                wait_alone(dve, dinv_ready, P + 1)
                for h in range(2):
                    t0 = P * NU + h * NB
                    dve.tensor_tensor(feat[:, bass.ds(t0, NB), 0, :], feat[:, bass.ds(t0, NB), 1, :],
                                      dinv[:, bass.ds(t0, NB), :].to_broadcast([128, NB, D]), ALU.mult)\
                       .then_inc(feat0_ready, 1)

            ring_sum(0, 0, first=True)
            ring_sum(0, 1)
            with dve.Fori(0, 2) as P:
                start_sums(P)
                sums(P * (NP - 1) + 1, NP - 2)
                diag_sums(P, P * ((NP - 1) * NS) + NP * NS)
                end_sums(P)
            with dve.Fori(2, NP - 1) as P:
                start_sums(P)
                sums(P * (NP - 1) + 1, NP - 1 - P)
                diag_sums(P, P * ((NP - 2) * NS) + (NP + 1) * NS)
                sums(P * (NP - 2) + NP, P - 1, P * NS + NS)
                end_sums(P)
            start_sums(NP - 1)
            diag_sums(NP - 1, ((NP - 1) * (NP - 2) + NP + 1) * NS)
            sums((NP - 1) * (NP - 1) + 1, NP - 2, NP * NS)
            end_sums(NP - 1, last=True)

            units = Tally(dve, "dve_units", NU)

            def split_lo(T, sweep, first=False, steps={}):
                u = 0 if first else units.now()
                chain.begin()
                for q in range(NU):
                    dve.wait_ge(hi_ready, u + (q + 1))
                    last = dve.tensor_tensor(a_lo[:, q % 4, :], ring[:, q // 2, q % 2, :],
                                             a_hi[:, q % 4, :].bitcast(f32), ALU.subtract)
                    if sweep == 2:
                        last = dve.tensor_tensor(f_parts[:, q % 4, 0, :, :], feat[:, bass.ds(T * NU + q, 1), :, :]
                                                 .rearrange("p o l f -> p (o l) f"),
                                                 f_parts[:, q % 4, 1, :, :].bitcast(f32), ALU.subtract)
                    last.then_inc(lo_ready, 1)
                    for step in steps.get(q, ()):
                        step(u)
                chain.end()
                if not first:
                    units.add(NU)

            def norm_stats(h, rows):
                for b in range(NB):
                    last = dve.bn_stats(stats[:, h, b, :], rows(b))
                chain.link(last, wait_alone)
                for b in range(NB):
                    last = dve.bn_aggr(mv[:, h, b, :], stats[:, h, b, :])
                last.then_inc(var_ready, 1)

            def normalize(h, rows, to, at):
                dve.wait_ge(rstd_ready, at)
                for b in range(NB):
                    last = dve.tensor_scalar(to(b), rows(b), mv[:, h, b, 0:1], rstd[:, h, b, :],
                                             ALU.subtract, ALU.mult)
                return last

            def tall_step(P, h, p):
                def step(u):
                    wait_alone(dve, done[0][h], u)
                    dve.tensor_tensor(tall[:, h, :], part[:, bass.ds(P * W + h * HALF, HALF)], acc0[h][:, :],
                                      ALU.add).then_inc(tall_ready[h], 1)
                return step

            def rows_step(P, h, p):
                def step(u):
                    t0 = P * NU + h * NB
                    yh = y[:, h, :, :]
                    dve.wait_ge(turned[h], p + 1)
                    ins = dve.tensor_tensor(yh, feat[:, bass.ds(t0, NB), 0, :],
                                            tr[h][:, :].rearrange("p (b f) -> p b f", b=NB), ALU.add)
                    chain.link(ins)
                    ins = dve.tensor_tensor(yh, yh, dinv[:, bass.ds(t0, NB), :].to_broadcast([128, NB, D]), ALU.mult)
                    ins.then_inc(turned_used[h], 1)
                    dve.wait_ge(turned_used[h], p + 1)
                    dve.wait_ge(xin_in, p * 16 + 16)
                    chain.link(dve.tensor_tensor(yh, yh, xin[:, h * NB:(h + 1) * NB, :], ALU.add))
                    norm_stats(h, lambda b: y[:, h, b, :])
                return step

            def x1_step(P, h, p):
                def step(u):
                    t0 = P * NU + h * NB
                    normalize(h, lambda b: y[:, h, b, :],
                              lambda b: feat[:, bass.ds(t0 + b, 1), 1, :].rearrange("p o f -> p (o f)"),
                              p * 2 + (h + 1)).then_inc(feat1_ready, 1)
                return step

            def layer0_steps(P, p):
                return {1: [tall_step(P, 0, p), tall_step(P, 1, p)], 3: [rows_step(P, 0, p)],
                        4: [x1_step(P, 0, p)], 5: [rows_step(P, 1, p)], 6: [x1_step(P, 1, p)]}

            dve.wait_ge(feat0_ready, 2 * NP)
            chain.begin()
            for h in range(2):
                dve.wait_ge(part_ready, 2 * NP)
                cols = slice((NP - 1) * W + h * HALF, (NP - 1) * W + (h + 1) * HALF)
                ins = dve.tensor_copy(tall[:, h, :], part[:, cols])
                ins.then_inc(tall_ready[h], 1)
                dve.wait_ge(tall_ready[h], 1)
                chain.link(dve.memset(part[:, cols], 0.0))
            for step in (rows_step, x1_step):
                for h in range(2):
                    step(NP - 1, h, 0)(0)
            chain.end()
            dve.wait_ge(feat1_ready, 2)
            split_lo(NP - 1, 2, first=True)
            with dve.Fori(0, NP - 2) as i:
                split_lo(NP - 1, 2, steps=layer0_steps(NP - 2 - i, i + 1))
                wait_alone(dve, feat1_ready, i * 2 + 4)
                with dve.Fori(0, i + 1) as k:
                    split_lo(NP - 2 - k, 2)

            def agg_step(P, h):
                def step(u):
                    wait_alone(dve, done[1][h], u)
                    half = part[:, bass.ds(P * W + h * HALF, HALF)]
                    dve.tensor_tensor(half, half, acc1[h][:, :], ALU.add).then_inc(agg_ready[h], 1)
                return step

            def npre_step(h, p):
                def step(u):
                    n = gn[:, h, :]
                    dve.wait_ge(rz_ready, p * 2 + (h + 1))
                    chain.link(dve.scalar_tensor_tensor(n, p_hn[:, :], bhh_s[:, 2:3], gr[:, h, :], ALU.add, ALU.mult))
                    dve.tensor_tensor(n, n, p_in[:, :], ALU.add).then_inc(npre_ready, 1)
                return step

            def sum_step(h, p):
                def step(u):
                    t = tall[:, h, :]
                    dve.wait_ge(x1t_ready, p * 2 + (h + 1))
                    dve.wait_ge(n_ready, p * 2 + (h + 1))
                    chain.link(dve.tensor_tensor(t, x1t[:, h, :], gn[:, h, :], ALU.subtract))
                    chain.link(dve.tensor_tensor(t, t, gz[:, h, :], ALU.mult))
                    dve.scalar_tensor_tensor(t, x1t[:, h, :], 2.0, t, ALU.mult, ALU.subtract).then_inc(sum_ready, 1)
                return step

            def new_row(h, b):
                return p_rows[h][:, b * 128:(b + 1) * 128]

            def out_stats_step(h, p):
                def step(u):
                    dve.wait_ge(rows_done, p * 2 + (h + 1))
                    norm_stats(h, lambda b: new_row(h, b))
                return step

            def out_step(h, p):
                def step(u):
                    normalize(h, lambda b: new_row(h, b), lambda b: y[:, h, b, :], p * 2 + (2 * NP + h + 1))\
                        .then_inc(rows_used, 1)
                return step

            def agg_steps(P):
                return {1: [agg_step(P, 0), agg_step(P, 1)]}

            def gru_steps(p):
                return {5: [npre_step(0, p)], 7: [sum_step(0, p)],
                        8: [npre_step(1, p)], 10: [sum_step(1, p), out_stats_step(0, p)], 11: [out_step(0, p)],
                        12: [out_stats_step(1, p)], 13: [out_step(1, p)]}

            def keep_lo_step(T, n):
                def step(u):
                    wait_alone(dve, x1_rounded, n + 1)
                    dve.tensor_tensor(feat[:, bass.ds(T * NU, NU), 0, :], feat[:, bass.ds(T * NU, NU), 1, :],
                                      rounded, ALU.subtract).then_inc(x1_lo_kept, 1)
                return step

            keep_lo_step(NP - 1, 0)(None)
            steps = layer0_steps(0, NP - 1)
            steps[4] = [keep_lo_step(NP - 2, 1)] + steps[4]
            split_lo(NP - 1, 3, steps=steps)
            dve.wait_ge(feat1_ready, 2 * NP)
            with dve.Fori(0, NP - 2) as k:
                split_lo(NP - 2 - k, 3, steps={4: [keep_lo_step(NP - 3 - k, k + 2)]})
            split_lo(0, 3)
            split_lo(0, 3, steps=agg_steps(NP - 1) | part1(gru_steps(0)))
            split_lo(NP - 2, 3, steps=agg_steps(0) | part2(gru_steps(0)))
            split_lo(NP - 3, 3, steps=part1(gru_steps(1)))
            split_lo(NP - 4, 3, steps=part2(gru_steps(1)))
            with dve.Fori(0, NP - 4) as k:
                split_lo(NP - 5 - k, 3)
            with dve.Fori(0, NP - 4) as i:
                split_lo(NP - 3 - i, 3, steps=agg_steps(NP - 2 - i) | part1(gru_steps(i + 2)))
                split_lo(NP - 4 - i, 3, steps=part2(gru_steps(i + 2)))
                with dve.Fori(i, NP - 4) as k:
                    split_lo(NP - 5 - k, 3)
            split_lo(1, 3, steps=agg_steps(2) | part1(gru_steps(NP - 2)))
            split_lo(0, 3, steps=part2(gru_steps(NP - 2)))
            u = units.now()
            chain.begin()
            for step in tail(agg_steps(1), gru_steps(NP - 1)):
                step(u)
            chain.end()

        @block.gpsimd
        def _(pool):
            pool.memset(ident[:, :], 0.0).then_inc(consts, 0 + 1)
            pool.wait_ge(consts, 1)
            pool.affine_select(out=ident[:, :], in_=ident[:, :], compare_op=ALU.not_equal, fill=1.0,
                               base=0, pattern=[[-1, 128]], channel_multiplier=1).then_inc(consts, 1)
            pool.wait_ge(zeroed, 4)
            pool.wait_ge(sum_done, NS)

            def load_xt(P, s):
                pool.dma_start(xt[:, s, :], x_t[:, bass.ds(P * W, W)]).then_inc(xt_in[s], 16)

            load_xt(0, 0)
            load_xt(1, 1)
            with pool.Fori(1, NP // 2) as i:
                for s in range(2):
                    wait_alone(pool, supp_done, i * 2 + (s - 1))
                    load_xt(i * 2 + s, s)
            with pool.Fori(0, NP) as P:
                pool.wait_ge(deg_ready, P + 1)
                pool.tensor_tensor(dinv[:, bass.ds(P * NU, NU), :], deg[:, :, :], mhalf[:, :, :], ALU.pow)\
                    .then_inc(dinv_ready, 1)

            def deviation(h, at):
                pool.wait_ge(var_ready, at)
                pool.tensor_tensor(var[:, h, :, :], mv[:, h, :, 1:2], eps_ln[:, 0:NB, :], ALU.add).then_inc(veps_ready, 1)
                pool.wait_ge(veps_ready, at)
                pool.tensor_tensor(rstd[:, h, :, :], var[:, h, :, :], mhalf[:, 0:NB, :], ALU.pow).then_inc(rstd_ready, 1)

            with pool.Fori(0, NP) as p:
                pool.dma_start(xin[:, :, :], x_rows[:, bass.ds((NP - 1 - p) * NU, NU), :]).then_inc(xin_in, 16)
                for h in range(2):
                    deviation(h, p * 2 + (h + 1))
            pool.wait_ge(x1_hi_kept, NP)

            def layer1(P, p):
                for h in range(2):
                    t0 = P * NU + h * NB
                    pool.tensor_tensor(xin[:, h * NB:(h + 1) * NB, :], feat[:, bass.ds(t0, NB), 0, :],
                                       feat[:, bass.ds(t0, NB), 1, :], ALU.add).then_inc(x1_ready, 1)
                for h in range(2):
                    deviation(h, p * 2 + (2 * NP + h + 1))
                    pool.wait_ge(rows_used, p * 2 + (h + 1))
                    pool.dma_start(out_rows[:, bass.ds(P * NU + h * NB, NB), :], y[:, h, :, :])\
                        .then_inc(stored[h], 16)
                for h in range(2):
                    wait_alone(pool, stored[h], p * 16 + 16)

            layer1(NP - 1, 0)
            layer1(0, 1)
            with pool.Fori(0, NP - 2) as i:
                layer1(NP - 2 - i, i + 2)


def kernel(x, adj, L0_gnn_weight, L1_gnn_W_msg, L1_gnn_b_msg, L1_gnn_W_ih, L1_gnn_W_hh, L1_gnn_b_ih, L1_gnn_b_hh):
    import numpy as np
    import concourse.bacc as bacc
    from concourse.bass_utils import run_bass_kernel_spmd

    W, NP, D = 1024, 8, 128
    a = np.asarray(adj).reshape(NP, W, NP, 4, 2, 128).transpose(0, 2, 3, 5, 4, 1)
    blocks = np.empty((NP * NP, 4, 128, 2, W), a.dtype)
    for P in range(NP):
        for k in range(NP):
            blocks[P * NP + k] = a[P, (P - k) % NP]
    c = np.ascontiguousarray
    arrays = {
        "adj_blocks": blocks,
        "x_t": c(np.asarray(x).T),
        "x": c(np.asarray(x)),
        "w0": c(np.asarray(L0_gnn_weight)),
        "wmsg_t": c(np.asarray(L1_gnn_W_msg).T),
        "b_msg": c(np.asarray(L1_gnn_b_msg).reshape(1, D).T),
        "wih_t": c(np.asarray(L1_gnn_W_ih).T),
        "whh_t": c(np.asarray(L1_gnn_W_hh).T),
        "b_ih": c(np.asarray(L1_gnn_b_ih).reshape(3, D).T),
        "b_hh": c(np.asarray(L1_gnn_b_hh).reshape(3, D).T),
    }
    nc = bacc.Bacc("TRN2", target_bir_lowering=False, num_devices=1)
    aps = {n: nc.dram_tensor(n, v.shape, mybir.dt.from_np(v.dtype), kind="ExternalInput").ap()
           for n, v in arrays.items()}
    out = nc.dram_tensor("out", (NP * W, D), mybir.dt.float32, kind="ExternalOutput").ap()
    gnn_resnorm_kernel(nc, **aps, out=out)
    return run_bass_kernel_spmd(nc, [arrays], core_ids=[0]).results[0]["out"]
```
